# Optimizing a Trainium2 kernel written in Bass

```python
import numpy as np
import jax
import jax.numpy as jnp

def _softmax(x, axis=-1):
    return jax.nn.softmax(x, axis=axis)

def _gelu(x):
    return jax.nn.gelu(x, approximate=True)

def _silu(x):
    return jax.nn.silu(x)

def _sigmoid(x):
    return jax.nn.sigmoid(x)

def _layernorm(x, axis=-1, eps=1e-05):
    m = jnp.mean(x, axis=axis, keepdims=True)
    v = jnp.var(x, axis=axis, keepdims=True)
    return (x - m) / jnp.sqrt(v + eps)

def _scatter_add(tgt, idx, src, axis=0):
    return tgt.at[idx].add(src)

def _segment_sum(src, seg, n):
    return jax.ops.segment_sum(src, seg, n)
kernel_name = 'mk_adj_ffn_d1_adj_r2_14ccc6'

def setup_inputs(seed: int=0):
    np.random.seed(seed)
    _w = jnp.asarray

    def _rec_inputs():
        import jax
        import jax.numpy as jnp
        _gk = jax.random.key(seed)
        x = -0.0005207 + 1.001 * jax.random.normal(jax.random.fold_in(_gk, 1), (4096, 128), jnp.float32)
        _a = jax.random.bernoulli(jax.random.fold_in(_gk, 2), 0.00390625, (4096, 4096))
        _a = jnp.logical_or(_a, jnp.swapaxes(_a, -1, -2))
        _a = jnp.logical_or(_a, jnp.eye(4096, dtype=bool))
        adj = _a.astype(jnp.int32)
        return (x, adj)
    x, adj = _rec_inputs()

    def _L0_gnn_setup():
        import jax, jax.numpy as jnp
        import numpy as np
        N, F_IN, F_OUT = (4096, 128, 128)
        ALPHA = 0.2
        NEG = -9000000000000000.0
        key = jax.random.key(seed)
        k1, k2, k3, k4, k5 = jax.random.split(key, 5)
        h = jax.random.normal(k1, (N, F_IN), dtype=jnp.float32)
        adj = jax.random.randint(k2, (N, N), 0, 2, dtype=jnp.int32)
        W_w = jax.random.normal(k3, (F_IN, F_OUT), dtype=jnp.float32) / np.sqrt(F_IN)
        W_b = jax.random.normal(k4, (F_OUT,), dtype=jnp.float32) * 0.01
        a = jax.random.normal(k5, (2 * F_OUT, 1), dtype=jnp.float32) / np.sqrt(2 * F_OUT)
        return {'h': h, 'adj': adj, 'W_w': W_w, 'W_b': W_b, 'a': a}
    _L0_gnn_all = _L0_gnn_setup()
    _L0_gnn_in = {k: v for k, v in _L0_gnn_all.items() if k in ('W_w', 'W_b', 'a')}
    del _L0_gnn_all

    def _L0_ffn_setup():
        import jax, jax.numpy as jnp
        import numpy as np
        B, S, D, H, E, K = (8, 4096, 128, 512, 8, 2)
        key = jax.random.key(seed)
        ks = jax.random.split(key, 7)
        s_in = 1.0 / np.sqrt(D)
        s_hid = 1.0 / np.sqrt(H)
        return {'x': jax.random.normal(ks[0], (B, S, D), dtype=jnp.float32), 'Wg': jax.random.uniform(ks[1], (E, D), jnp.float32, -s_in, s_in), 'bg': jax.random.uniform(ks[2], (E,), jnp.float32, -s_in, s_in), 'W1': jax.random.uniform(ks[3], (E, H, D), jnp.float32, -s_in, s_in), 'b1': jax.random.uniform(ks[4], (E, H), jnp.float32, -s_in, s_in), 'W2': jax.random.uniform(ks[5], (E, D, H), jnp.float32, -s_hid, s_hid), 'b2': jax.random.uniform(ks[6], (E, D), jnp.float32, -s_hid, s_hid)}
    _L0_ffn_all = _L0_ffn_setup()
    _L0_ffn_in = {k: v for k, v in _L0_ffn_all.items() if k in ('Wg', 'bg', 'W1', 'b1', 'W2', 'b2')}
    del _L0_ffn_all
    return {'x': x, 'adj': adj, 'L0_gnn_W_w': _L0_gnn_in['W_w'], 'L0_gnn_W_b': _L0_gnn_in['W_b'], 'L0_gnn_a': _L0_gnn_in['a'], 'L0_ffn_Wg': _L0_ffn_in['Wg'], 'L0_ffn_bg': _L0_ffn_in['bg'], 'L0_ffn_W1': _L0_ffn_in['W1'], 'L0_ffn_b1': _L0_ffn_in['b1'], 'L0_ffn_W2': _L0_ffn_in['W2'], 'L0_ffn_b2': _L0_ffn_in['b2']}

def reference(x, adj, L0_gnn_W_w, L0_gnn_W_b, L0_gnn_a, L0_ffn_Wg, L0_ffn_bg, L0_ffn_W1, L0_ffn_b1, L0_ffn_W2, L0_ffn_b2):
    import jax
    import jax.numpy as jnp

    def _L0_gnn_ref(h, adj, W_w, W_b, a):
        import jax, jax.numpy as jnp
        import numpy as np
        N, F_IN, F_OUT = (4096, 128, 128)
        ALPHA = 0.2
        NEG = -9000000000000000.0
        Wh = h @ W_w + W_b
        a1 = a[:F_OUT, 0]
        a2 = a[F_OUT:, 0]
        e = jax.nn.leaky_relu((Wh @ a1)[:, None] + (Wh @ a2)[None, :], negative_slope=ALPHA)
        attention = jnp.where(adj > 0, e, NEG)
        attention = jax.nn.softmax(attention, axis=1)
        h_prime = attention @ Wh
        return h_prime

    def _L0_ffn_ref(x, Wg, bg, W1, b1, W2, b2):
        import jax, jax.numpy as jnp
        import numpy as np
        B, S, D, H, E, K = (8, 4096, 128, 512, 8, 2)
        gate_scores = jnp.einsum('bsd,ed->bse', x, Wg) + bg
        topk_scores, topk_idx = jax.lax.top_k(gate_scores, K)
        topk_probs = jax.nn.softmax(topk_scores, axis=-1)
        combine = jnp.sum(topk_probs[..., None] * jax.nn.one_hot(topk_idx, E, dtype=x.dtype), axis=-2)
        out = jnp.zeros_like(x)
        for e in range(E):
            h = jax.nn.relu(jnp.einsum('bsd,hd->bsh', x, W1[e]) + b1[e])
            y = jnp.einsum('bsh,dh->bsd', h, W2[e]) + b2[e]
            out = out + combine[..., e:e + 1] * y
        return out
    x = x + _L0_gnn_ref(_layernorm(x, axis=-1), adj, L0_gnn_W_w, L0_gnn_W_b, L0_gnn_a)
    x = x + _L0_ffn_ref(_layernorm(x, axis=-1)[None], L0_ffn_Wg, L0_ffn_bg, L0_ffn_W1, L0_ffn_b1, L0_ffn_W2, L0_ffn_b2)[0]
    return x

_drawn_inputs = setup_inputs


def setup_inputs(seed=0):
    import zlib

    import numpy as np

    out = dict(_drawn_inputs(seed))
    spreads = {}
    factors = {'L0_gnn_W_b': 3.308, 'L0_ffn_b1': 3.92, 'L0_ffn_b2': 3.121}
    for name, (base, spread) in spreads.items():
        noise = np.random.default_rng([zlib.crc32(name.encode()), seed]).standard_normal(out[name].shape)
        drawn = base * np.exp(spread * noise) if base else spread * noise
        out[name] = jnp.asarray(drawn.astype(out[name].dtype))
    for name, factor in factors.items():
        out[name] = (out[name] * factor).astype(out[name].dtype)
    return out
```

```python
import concourse.bass as bass
from concourse import mybir
from contextlib import ExitStack


def build(nc, x, adj, W, Wb, a, WgT, bg, w1, b1, w2, b2, out):
    fp32, i32, u32 = mybir.dt.float32, mybir.dt.int32, mybir.dt.uint32
    ALU = mybir.AluOpType
    ACT = mybir.ActivationFunctionType
    X = mybir.AxisListType.X

    N, F = x.shape
    E = WgT.shape[1]
    HID = w1.shape[1] // E
    P = 128
    TILES = N // P
    GT = 4
    GROUPS = TILES // GT
    GW = GT * P
    KH = HID // P
    CH = 8
    CW = N // CH
    QC = 4
    QW = N // QC
    EPS = 1e-5
    SLOPE = 0.2
    UNIT = 2.0 ** -50
    NFIN = 13
    assert E == 2 * GT and KH == 4

    ctx = ExitStack()
    with ctx:
        def sb(name, shape, dt=fp32):
            return ctx.enter_context(nc.sbuf_tensor(name, shape, dt))

        def pb(name, shape=(P, 512)):
            return ctx.enter_context(nc.psum_tensor(name, list(shape), fp32))

        def sem(name):
            return ctx.enter_context(nc.semaphore(name))

        rows = [sb(f"rows{i}", [P, N], i32) for i in range(GT)]
        prob = [r[:, :].bitcast(fp32) for r in rows]
        t_bc = sb("t_bc", [P, N])
        v_bc = sb("v_bc", [P, N])
        q = sb("q", [P, QC, QW])
        Wh = sb("Wh", [P, TILES, F])
        w1_sb = sb("w1_sb", [P, E * HID])
        w2_sb = sb("w2_sb", [P, E, KH, F])
        pt = [sb(f"pt{i}", [P, CW]) for i in range(4)]
        h = [sb(f"h{i}", [P, KH, GW]) for i in range(2)]
        ident = sb("ident", [P, P])
        ones = sb("ones", [P, P])
        W_sb = sb("W_sb", [P, F])
        a_sb = sb("a_sb", [P, 2])
        a2_bc = sb("a2_bc", [P, P])
        Wb_row = sb("Wb_row", [P, F])
        Wb_col = sb("Wb_col", [P, 1])
        WgT_sb = sb("WgT_sb", [P, E])
        bg_bc = sb("bg_bc", [P, E])
        b1_sb = sb("b1_sb", [P, E * KH])
        b2_sb = sb("b2_sb", [E, F])
        lane = sb("lane", [P, E])
        mhalf = sb("mhalf", [P, 1])
        whT = [h[0][:, i, :] for i in range(2)]
        hT = [h[0][:, 2 + i, :] for i in range(2)]
        sq = sb("sq", [P, TILES])
        tmax = sb("tmax", [P, 1])
        st0 = sb("st0", [P, TILES, 6])
        mv0 = sb("mv0", [P, TILES, 2])
        rs0 = sb("rs0", [P, TILES])
        mx = sb("mx", [P, QC])
        mneg = sb("mneg", [P, 1])
        nbias = sb("nbias", [P, GT])
        dparts = sb("dparts", [P, GT, QC])
        xt = sb("xt", [P, GT, F])
        x1n = sb("x1n", [P, GT, F])
        xnTn = sb("xnTn", [P, GW])
        combn = sb("combn", [P, GT, E])
        yacc = sb("yacc", [P, GT, F])
        xnTc = sb("xnTc", [P, GW])
        combc = sb("combc", [P, GT, E])
        ot = sb("ot", [P, GT, F])
        xn = sb("xn", [P, F])
        den = sb("den", [P, 1])
        rden = sb("rden", [P, 1])
        st = sb("st", [P, 6])
        mv = sb("mv", [P, 2])
        ve = sb("ve", [P, 1])
        rstd = sb("rstd", [P, 1])
        gs = sb("gs", [P, E])
        m8 = sb("m8", [P, 8])
        ix = sb("ix", [P, 8], u32)
        ixf = sb("ixf", [P, 2])
        gd = sb("gd", [P, 1])
        ed = sb("ed", [P, 1])
        eq = sb("eq", [P, 1])
        p1 = sb("p1", [P, 1])
        p2 = sb("p2", [P, 1])
        c1 = sb("c1", [P, E])
        c2 = sb("c2", [P, E])
        idle = sb("idle", [1, 1])
        srow = sb("srow", [P, GT])
        combT = sb("combT", [E, P])
        xin = rows[2][:, :].bitcast(fp32).rearrange("p (c f) -> p c f", f=F)
        xh = rows[3][:, :].bitcast(fp32).rearrange("p (c f) -> p c f", f=F)

        tp = [pb(f"tp{i}") for i in range(2)]
        hps = [pb(f"hps{i}") for i in range(2)]
        yps = [pb(f"yps{i}") for i in range(2)]
        acc = pb("acc")
        misc = pb("misc")

        s_wa = sem("s_wa")
        s_we = sem("s_we")
        s_xin = sem("s_xin")
        s_adj = [sem(f"s_adj{i}") for i in range(GT)]
        s_xt = [sem(f"s_xt{i}") for i in range(GT)]
        s_zero = sem("s_zero")
        s_const = sem("s_const")
        s_pl = sem("s_pl")
        s_var0 = sem("s_var0")
        s_sd0 = sem("s_sd0")
        s_xh = sem("s_xh")
        s_t0 = sem("s_t0")
        s_hT = sem("s_hT")
        s_whT = sem("s_whT")
        s_whTs = sem("s_whTs")
        s_wh = sem("s_wh")
        s_whs = sem("s_whs")
        s_ts = sem("s_ts")
        s_tse = sem("s_tse")
        s_pre = sem("s_pre")
        s_srow = sem("s_srow")
        s_v = sem("s_v")
        s_q = sem("s_q")
        s_w = sem("s_w")
        s_mneg = sem("s_mneg")
        s_nb = sem("s_nb")
        s_p = sem("s_p")
        s_trans = sem("s_trans")
        s_ev = [sem("s_evv"), sem("s_eva")]
        s_am = sem("s_am")
        s_fin = sem("s_fin")
        s_x1 = sem("s_x1")
        s_ve = sem("s_ve")
        s_rstd = sem("s_rstd")
        s_xn = sem("s_xn")
        s_xtp = sem("s_xtp")
        s_xnt = sem("s_xnt")
        s_gate = sem("s_gate")
        s_gd = sem("s_gd")
        s_ed = sem("s_ed")
        s_comb = sem("s_comb")
        s_ctp = sem("s_ctp")
        s_cT = sem("s_cT")
        s_bias = sem("s_bias")
        s_res = sem("s_res")
        s_cpx = sem("s_cpx")
        s_cpc = sem("s_cpc")
        s_h = sem("s_h")
        s_relu = sem("s_relu")
        s_y = sem("s_y")
        s_cb = sem("s_cb")
        s_out = sem("s_out")

        def ge(eng, s, value):
            if not (isinstance(value, int) and value <= 0):
                eng.wait_ge(s, value)

        def bodies(eng, steps):
            steps(-1)
            steps(0)
            steps(1)
            with eng.Fori(2, GROUPS - 1) as g:
                steps(g)
            steps(GROUPS - 1)
            steps(GROUPS)

        def has_tile(g, t):
            return not isinstance(g, int) or 0 <= GT * g + t < TILES

        def has_experts(g):
            return not isinstance(g, int) or 1 <= g <= GROUPS

        block = ctx.enter_context(nc.Block())

        @block.sync
        def _(sp):
            sp.dma_start(xin, x.rearrange("(c p) f -> p c f", p=P)).then_inc(s_xin, 16)
            sp.dma_start(W_sb[:, :], W).then_inc(s_wa, 16)
            sp.dma_start(a_sb[:, 0:1], a[0:F, :]).then_inc(s_wa, 16)
            sp.dma_start(a_sb[:, 1:2], a[F:2 * F, :]).then_inc(s_wa, 16)
            sp.dma_start(Wb_row[:, :], Wb[0:1, :].broadcast_to([P, F])).then_inc(s_wa, 16)
            sp.dma_start(Wb_col[:, :], Wb.rearrange("a f -> f a")).then_inc(s_wa, 16)
            for t in range(2):
                sp.dma_start(rows[t][:, :], adj[t * P:(t + 1) * P, :]).then_inc(s_adj[t], 16)
            sp.dma_start(WgT_sb[:, :], WgT).then_inc(s_we, 16)
            sp.dma_start(bg_bc[:, :], bg[0:1, :].broadcast_to([P, E])).then_inc(s_we, 16)
            sp.dma_start(b1_sb[:, :], b1).then_inc(s_we, 16)
            sp.dma_start(b2_sb[:, :], b2).then_inc(s_we, 16)
            sp.dma_start(w1_sb[:, :], w1).then_inc(s_we, 16)
            sp.dma_start(w2_sb[:, :, :, :], w2).then_inc(s_we, 16)
            sp.wait_ge(s_t0, GROUPS)
            for t in range(2, GT):
                sp.dma_start(rows[t][:, :], adj[t * P:(t + 1) * P, :]).then_inc(s_adj[t], 16)
            for t in range(GT):
                sp.dma_start(xt[:, t, :], x[t * P:(t + 1) * P, :]).then_inc(s_xt[t], 16)

            def load_group(g):
                for t in range(GT):
                    sp.wait_ge(s_trans, CH * (GT * g + t - GT + 1))
                    sp.dma_start(rows[t][:, :], adj[bass.ds((GT * g + t) * P, P), :]).then_inc(s_adj[t], 16)
                    sp.wait_ge(s_x1, GT * g + t - GT + 1)
                    sp.dma_start(xt[:, t, :], x[bass.ds((GT * g + t) * P, P), :]).then_inc(s_xt[t], 16)

            def store_group(n):
                sp.wait_ge(s_cb, E * (n + 1))
                sp.dma_start(out[bass.ds(n * GW, GW), :].rearrange("(c p) f -> p c f", p=P),
                             ot[:, :, :]).then_inc(s_out, 16)

            load_group(1)
            with sp.Fori(2, GROUPS) as g:
                load_group(g)
                store_group(g - 2)
            store_group(GROUPS - 2)
            store_group(GROUPS - 1)
            sp.wait_ge(s_out, 16 * GROUPS)

        @block.gpsimd
        def _(pool):
            nc.gpsimd.memset(ident[:, :], 0.0).then_inc(s_zero, 1)
            nc.gpsimd.memset(ones[:, :], 1.0).then_inc(s_const, 1)
            nc.gpsimd.memset(mhalf[:, :], -0.5).then_inc(s_const, 1)
            nc.gpsimd.iota(lane[:, :], [[1, E]], base=0, channel_multiplier=0,
                           allow_small_or_imprecise_dtypes=True).then_inc(s_const, 1)
            pool.wait_ge(s_zero, 1)
            nc.gpsimd.affine_select(out=ident[:, :], in_=ident[:, :], compare_op=ALU.not_equal, fill=1.0,
                                    base=0, pattern=[[-1, P]], channel_multiplier=1).then_inc(s_const, 1)
            pool.wait_ge(s_const, 4)
            with pool.Fori(0, TILES) as T:
                pool.wait_ge(s_ve, T + 1)
                nc.gpsimd.tensor_tensor(rstd[:, :], ve[:, :], mhalf[:, :], ALU.pow).then_inc(s_rstd, 1)

        @block.vector
        def _(dve):
            links = [0]

            def link(ins):
                links[0] += 1
                ins.then_inc(s_pl, 1)
                dve.wait_ge(s_pl, links[0])

            dve.wait_ge(s_xin, 16)
            for c in range(TILES):
                last = nc.vector.bn_stats(st0[:, c, :], xin[:, c, :])
            link(last)
            for c in range(TILES):
                last = nc.vector.bn_aggr(mv0[:, c, :], st0[:, c, :])
            link(last)
            nc.vector.tensor_scalar(rs0[:, :], mv0[:, :, 1], EPS, None, ALU.add).then_inc(s_var0, 1)
            dve.wait_ge(s_sd0, 1)
            link(nc.vector.reciprocal(rs0[:, :], rs0[:, :]))
            for c in range(TILES):
                ins = nc.vector.tensor_scalar(xh[:, c, :], xin[:, c, :], mv0[:, c, 0:1], rs0[:, c:c + 1],
                                              ALU.subtract, ALU.mult)
                if c % GT == GT - 1:
                    ins.then_inc(s_xh, 1)
            dve.wait_ge(s_const, 4)
            dve.wait_ge(s_wa, 80)
            nc.vector.tensor_scalar(a2_bc[:, :], ones[:, :], a_sb[:, 1:2], None, ALU.mult).then_inc(s_pre, 1)
            for g in range(GROUPS):
                dve.wait_ge(s_wh, g + 1)
                for b in range(GT):
                    last = nc.vector.tensor_tensor(Wh[:, GT * g + b, :], yps[g % 2][:, b * P:(b + 1) * P],
                                                   Wb_row[:, :], ALU.add)
                last.then_inc(s_whs, 1)
                dve.wait_ge(s_ts, g + 1)
                nc.vector.tensor_copy(t_bc[:, g * GW:(g + 1) * GW], tp[g % 2][:, :])
                nc.vector.tensor_scalar(sq[:, GT * g:GT * (g + 1)], acc[:, 8 * g:8 * g + GT],
                                        (1.0 - SLOPE) * UNIT, None, ALU.mult).then_inc(s_tse, 1)
            dve.wait_ge(s_tse, GROUPS)
            link(nc.vector.tensor_reduce(tmax[:, :], t_bc[:, :], X, ALU.max))
            nc.vector.tensor_scalar(v_bc[:, :], t_bc[:, :], tmax[:, :], -SLOPE * UNIT,
                                    ALU.subtract, ALU.mult).then_inc(s_pre, 1)
            dve.wait_ge(s_pre, 2)

            def gate():
                nc.vector.memset(idle[:, :], 0.0)

            def make_v(g, t, c):
                s = t % GT
                if c == 0:
                    nc.vector.tensor_scalar(srow[:, s:s + 1], sq[:, bass.ds(GT * g + t, 1)], 1.0, None,
                                            ALU.mult).then_inc(s_srow, 1)
                    dve.wait_ge(s_adj[s], 16 * (g + t // GT + 1))
                cols = slice(c * QW, (c + 1) * QW)
                nc.vector.scalar_tensor_tensor(prob[s][:, cols], rows[s][:, cols], 0.0, v_bc[:, cols],
                                               op0=ALU.is_le, op1=ALU.max).then_inc(s_v, 1)

            def make_w(g, t, c):
                s, T = t % GT, GT * g + t
                cols = slice(c * QW, (c + 1) * QW)
                dve.wait_ge(s_v, QC * T + c + 1)
                dve.wait_ge(s_q, QC * T + c + 1)
                if c == 0:
                    ge(dve, s_mneg, T)
                gate()
                nc.vector.tensor_tensor_reduce(out=prob[s][:, cols], in0=q[:, c, :], in1=prob[s][:, cols],
                                               scale=1.0, scalar=-3.0e38, op0=ALU.subtract, op1=ALU.max,
                                               accum_out=mx[:, c:c + 1]).then_inc(s_w, 1)

            def make_bias(g, t):
                s, T = t % GT, GT * g + t
                dve.wait_ge(s_w, QC * (T + 1))
                ge(dve, s_nb, T)
                nc.vector.tensor_reduce(mneg[:, :], mx[:, :], X, ALU.max, negate=True).then_inc(s_mneg, 1)
                dve.wait_ge(s_mneg, T + 1)
                ge(dve, s_p, QC * (T - GT + 1))
                nc.vector.tensor_scalar(nbias[:, s:s + 1], mneg[:, :], 1.0 / UNIT, None,
                                        ALU.mult).then_inc(s_nb, 1)

            def evacuate(g, t, c):
                T = GT * g + t
                dve.wait_ge(s_trans, CH * T + c + 1)
                ge(dve, s_am, CH * T + c - 3)
                nc.vector.tensor_copy(pt[c % 4][:, :], tp[0][:, :]).then_inc(s_ev[0], 1)

            def finish(g, t, part):
                s, T = t % GT, GT * g + t
                n = [0]

                def after(k):
                    dve.wait_ge(s_fin, NFIN * T + k)

                if part == 0:
                    dve.wait_ge(s_p, QC * (T + 1))
                    nc.vector.tensor_reduce(den[:, :], dparts[:, s, :], X, ALU.add).then_inc(s_fin, 1)
                    after(1)
                    nc.vector.reciprocal(rden[:, :], den[:, :]).then_inc(s_fin, 1)
                    dve.wait_ge(s_am, CH * (T + 1))
                    dve.wait_ge(s_xt[s], 16 * (g + t // GT + 1))
                    after(2)
                    nc.vector.scalar_tensor_tensor(x1n[:, s, :], acc[:, 0:F], rden[:, :], xt[:, s, :],
                                                   op0=ALU.mult, op1=ALU.add).then_inc(s_x1, 1)
                    dve.wait_ge(s_x1, T + 1)
                    nc.vector.bn_stats(st[:, :], x1n[:, s, :]).then_inc(s_fin, 1)
                    after(3)
                    gate()
                    nc.vector.bn_aggr(mv[:, :], st[:, :]).then_inc(s_fin, 1)
                    after(4)
                    nc.vector.tensor_scalar(ve[:, :], mv[:, 1:2], EPS, None, ALU.add).then_inc(s_ve, 1)
                if part == 1:
                    dve.wait_ge(s_rstd, T + 1)
                    ge(dve, s_xtp, T)
                    nc.vector.tensor_scalar(xn[:, :], x1n[:, s, :], mv[:, 0:1], rstd[:, :],
                                            ALU.subtract, ALU.mult).then_inc(s_xn, 1)
                if part == 4:
                    dve.wait_ge(s_gate, T + 1)
                    nc.vector.tensor_tensor(gs[:, :], misc[:, F:F + E], bg_bc[:, :], ALU.add).then_inc(s_fin, 1)
                    after(5)
                    gate()
                    nc.vector.max(m8[:, :], gs[:, :]).then_inc(s_fin, 1)
                    after(6)
                    nc.vector.tensor_tensor(gd[:, :], m8[:, 1:2], m8[:, 0:1], ALU.subtract).then_inc(s_gd, 1)
                    nc.vector.max_index(ix[:, :], m8[:, :], gs[:, :]).then_inc(s_fin, 1)
                    after(7)
                    nc.vector.tensor_copy(ixf[:, :], ix[:, 0:2]).then_inc(s_fin, 1)
                if part == 5:
                    dve.wait_ge(s_ed, T + 1)
                    nc.vector.tensor_scalar(eq[:, :], ed[:, :], 1.0, None, ALU.add).then_inc(s_fin, 1)
                    after(9)
                    nc.vector.reciprocal(p1[:, :], eq[:, :]).then_inc(s_fin, 1)
                    after(10)
                    nc.vector.tensor_scalar(c1[:, :], lane[:, :], ixf[:, 0:1], p1[:, :],
                                            ALU.is_equal, ALU.mult).then_inc(s_fin, 1)
                    nc.vector.tensor_tensor(p2[:, :], ed[:, :], p1[:, :], ALU.mult).then_inc(s_fin, 1)
                    after(12)
                    nc.vector.tensor_scalar(c2[:, :], lane[:, :], ixf[:, 1:2], p2[:, :],
                                            ALU.is_equal, ALU.mult).then_inc(s_fin, 1)
                    after(13)
                    nc.vector.tensor_tensor(combn[:, s, :], c1[:, :], c2[:, :], ALU.add).then_inc(s_comb, 1)
                if part == 7:
                    dve.wait_ge(s_bias, T + 1)
                    nc.vector.tensor_tensor(x1n[:, s, :], x1n[:, s, :], misc[:, 2 * F:3 * F],
                                            ALU.add).then_inc(s_res, 1)

            def combine(g, e):
                n = E * (g - 1) + e
                dve.wait_ge(s_y, n + 1)
                ge(dve, s_cb, n)
                if e == 0:
                    dve.wait_ge(s_cpc, g)
                if e == E - 1:
                    ge(dve, s_out, 16 * (g - 1))
                dst = ot if e == E - 1 else yacc
                for b in range(GT):
                    last = nc.vector.scalar_tensor_tensor(
                        dst[:, b, :], yps[e % 2][:, b * P:(b + 1) * P], combc[:, b, e:e + 1],
                        yacc[:, b, :], op0=ALU.mult, op1=ALU.add)
                last.then_inc(s_cb, 1)

            def hand_over(g):
                dve.wait_ge(s_res, GT * (g + 1))
                dve.wait_ge(s_comb, GT * (g + 1))
                ge(dve, s_cb, E * g)
                nc.vector.tensor_copy(yacc[:, :, :], x1n[:, :, :])
                nc.vector.tensor_copy(combc[:, :, :], combn[:, :, :]).then_inc(s_cpc, 1)

            def steps(g):
                for r in range(1, GT + 1):
                    e0 = 2 * (r - 1)
                    for c in range(CH):
                        if has_experts(g) and e0 and c in (0, 4):
                            combine(g, e0 - 2 + c // 4)
                        if c % 2 == 0 and has_tile(g, r):
                            evacuate(g, r, c)
                        if c % 2 == 0 and has_tile(g, r + 2):
                            make_v(g, r + 2, c // 2)
                        if c % 2 == 1 and has_tile(g, r + 2):
                            make_w(g, r + 2, c // 2)
                        if has_tile(g, r - 1):
                            finish(g, r - 1, c)
                    if has_tile(g, r + 2):
                        make_bias(g, r + 2)
                if has_experts(g):
                    combine(g, E - 2)
                    combine(g, E - 1)
                if has_tile(g, GT - 1):
                    hand_over(g)

            bodies(dve, steps)

        @block.scalar
        def _(act):
            act.wait_ge(s_var0, 1)
            nc.scalar.activation(rs0[:, :], rs0[:, :], ACT.Sqrt).then_inc(s_sd0, 1)
            act.wait_ge(s_wa, 80)
            for g in range(GROUPS):
                act.wait_ge(s_t0, g + 1)
                if g >= 2:
                    act.wait_ge(s_wh, g - 1)
                nc.scalar.activation(hT[g % 2], hps[g % 2][:, :], ACT.Copy).then_inc(s_hT, 1)
                act.wait_ge(s_whT, g + 1)
                if g >= 2:
                    act.wait_ge(s_ts, g - 1)
                nc.scalar.activation(whT[g % 2], misc[:, :], ACT.Identity,
                                     bias=Wb_col[:, :]).then_inc(s_whTs, 1)
            act.wait_ge(s_tse, GROUPS)

            def make_q(g, t, c):
                s, T = t % GT, GT * g + t
                if c == 0:
                    act.wait_ge(s_srow, T + 1)
                ge(act, s_w, QC * (T - 1) + c + 1)
                nc.scalar.activation(q[:, c, :], t_bc[:, c * QW:(c + 1) * QW], ACT.Relu,
                                     bias=srow[:, s:s + 1], scale=(1.0 - SLOPE) * UNIT).then_inc(s_q, 1)

            def make_p(g, t, c):
                s, T = t % GT, GT * g + t
                if c == 0:
                    act.wait_ge(s_nb, T + 1)
                    ge(act, s_fin, NFIN * (T - GT) + 1)
                cols = slice(c * QW, (c + 1) * QW)
                nc.scalar.activation(prob[s][:, cols], prob[s][:, cols], ACT.Exp, bias=nbias[:, s:s + 1],
                                     scale=1.0 / UNIT, accum_out=dparts[:, s, c:c + 1]).then_inc(s_p, 1)

            def evacuate(g, t, c):
                T = GT * g + t
                act.wait_ge(s_trans, CH * T + c + 1)
                ge(act, s_am, CH * T + c - 3)
                nc.scalar.activation(pt[c % 4][:, :], tp[1][:, :], ACT.Copy).then_inc(s_ev[1], 1)

            def relu(g, e, k):
                n = KH * (E * (g - 1) + e) + k
                act.wait_ge(s_h, n + 1)
                ge(act, s_y, E * (g - 1) + e - 1)
                nc.scalar.activation(h[e % 2][:, k, :], hps[k % 2][:, :], ACT.Relu,
                                     bias=b1_sb[:, KH * e + k:KH * e + k + 1]).then_inc(s_relu, 1)

            def finish(g, t, part):
                s, T = t % GT, GT * g + t
                if part == 2:
                    act.wait_ge(s_xtp, T + 1)
                    if s == 0:
                        ge(act, s_cpx, g + t // GT)
                    nc.scalar.activation(xnTn[:, s * P:(s + 1) * P], misc[:, 0:P], ACT.Copy).then_inc(s_xnt, 1)
                if part == 4:
                    act.wait_ge(s_gd, T + 1)
                    nc.scalar.activation(ed[:, :], gd[:, :], ACT.Exp).then_inc(s_ed, 1)
                if part == 6:
                    act.wait_ge(s_ctp, T + 1)
                    nc.scalar.activation(combT[:, :], misc[0:E, 3 * F:3 * F + P], ACT.Copy).then_inc(s_cT, 1)

            def steps(g):
                for r in range(1, GT + 1):
                    e0 = 2 * (r - 1)
                    for c in range(CH):
                        if has_experts(g):
                            relu(g, e0 + c // KH, c % KH)
                        if c % 2 == 1 and has_tile(g, r):
                            evacuate(g, r, c)
                        if c % 2 == 0 and has_tile(g, r + 2):
                            make_q(g, r + 2, c // 2)
                        if has_tile(g, r - 1):
                            finish(g, r - 1, c)
                        if c % 2 == 1 and has_tile(g, r + 1):
                            make_p(g, r + 1, c // 2)
                if has_tile(g, GT - 1):
                    act.wait_ge(s_xnt, GT * (g + 1))
                    ge(act, s_h, KH * E * g)
                    nc.scalar.activation(xnTc[:, :], xnTn[:, :], ACT.Copy).then_inc(s_cpx, 1)

            bodies(act, steps)

        @block.tensor
        def _(pe):
            pe.wait_ge(s_const, 4)
            pe.wait_ge(s_wa, 80)
            for g in range(GROUPS):
                pe.wait_ge(s_xh, g + 1)
                if g >= 2:
                    pe.wait_ge(s_hT, g - 1)
                for b in range(GT):
                    last = nc.tensor.transpose(hps[g % 2][:, b * P:(b + 1) * P], xh[:, GT * g + b, :], ident[:, :])
                last.then_inc(s_t0, 1)
                pe.wait_ge(s_hT, g + 1)
                if g >= 1:
                    pe.wait_ge(s_whTs, g)
                nc.tensor.matmul(misc[:, :], W_sb[:, :], hT[g % 2], start=True, stop=True).then_inc(s_whT, 1)
                if g >= 2:
                    pe.wait_ge(s_whs, g - 1)
                for b in range(GT):
                    last = nc.tensor.matmul(yps[g % 2][:, b * P:(b + 1) * P], hT[g % 2][:, b * P:(b + 1) * P],
                                            W_sb[:, :], start=True, stop=True)
                last.then_inc(s_wh, 1)
                pe.wait_ge(s_whTs, g + 1)
                if g == 0:
                    pe.wait_ge(s_pre, 1)
                if g >= 1:
                    pe.wait_ge(s_tse, g)
                nc.tensor.matmul(tp[g % 2][:, :], a2_bc[:, :], whT[g % 2], start=True, stop=True)
                for b in range(GT):
                    last = nc.tensor.matmul(acc[:, 8 * g + b:8 * g + b + 1], whT[g % 2][:, b * P:(b + 1) * P],
                                            a_sb[:, 0:1], start=True, stop=True)
                last.then_inc(s_ts, 1)
            pe.wait_ge(s_tse, GROUPS)
            pe.wait_ge(s_whs, GROUPS)
            pe.wait_ge(s_we, 96)

            def transposes(g, t, c):
                s, T = t % GT, GT * g + t
                if c % 2 == 0:
                    pe.wait_ge(s_p, QC * T + c // 2 + 1)
                ge(pe, s_ev[c % 2], CH // 2 * T + c // 2)
                for b in range(CW // P):
                    j = c * CW + b * P
                    last = nc.tensor.transpose(tp[c % 2][:, b * P:(b + 1) * P], prob[s][:, j:j + P], ident[:, :])
                last.then_inc(s_trans, 1)

            def attend(g, t, c):
                T = GT * g + t
                pe.wait_ge(s_ev[c % 2], CH // 2 * T + c // 2 + 1)
                if c == 0:
                    ge(pe, s_x1, T)
                for b in range(CW // P):
                    last = nc.tensor.matmul(acc[:, 0:F], pt[c % 4][:, b * P:(b + 1) * P],
                                            Wh[:, CW // P * c + b, :], start=(c == 0 and b == 0),
                                            stop=(c == CH - 1 and b == CW // P - 1))
                last.then_inc(s_am, 1)

            def up(g, e, k):
                n = KH * (E * (g - 1) + e) + k
                if e == 0 and k == 0:
                    pe.wait_ge(s_cpx, g)
                ge(pe, s_relu, n - 1)
                j = e * HID + k * P
                nc.tensor.matmul(hps[k % 2][:, :], w1_sb[:, j:j + P], xnTc[:, :], start=True,
                                 stop=True).then_inc(s_h, 1)

            def down(g, e, b):
                n = E * (g - 1) + e
                if b == 0:
                    pe.wait_ge(s_relu, KH * (n + 1))
                    ge(pe, s_cb, n - 1)
                for k in range(KH):
                    last = nc.tensor.matmul(yps[e % 2][:, b * P:(b + 1) * P], h[e % 2][:, k, b * P:(b + 1) * P],
                                            w2_sb[:, e, k, :], start=(k == 0), stop=(k == KH - 1))
                if b == GT - 1:
                    last.then_inc(s_y, 1)

            def finish(g, t, part):
                s, T = t % GT, GT * g + t
                if part == 2:
                    pe.wait_ge(s_xn, T + 1)
                    ge(pe, s_res, T)
                    nc.tensor.transpose(misc[:, 0:P], xn[:, :], ident[:, :]).then_inc(s_xtp, 1)
                if part == 3:
                    pe.wait_ge(s_xnt, T + 1)
                    nc.tensor.matmul(misc[:, F:F + E], xnTn[:, s * P:(s + 1) * P], WgT_sb[:, :],
                                     start=True, stop=True).then_inc(s_gate, 1)
                if part == 6:
                    pe.wait_ge(s_comb, T + 1)
                    nc.tensor.transpose(misc[0:E, 3 * F:3 * F + P], combn[:, s, :], ident[:, :]).then_inc(s_ctp, 1)
                if part == 7:
                    pe.wait_ge(s_cT, T + 1)
                    nc.tensor.matmul(misc[:, 2 * F:3 * F], combT[:, :], b2_sb[:, :], start=True,
                                     stop=True).then_inc(s_bias, 1)

            def steps(g):
                for r in range(1, GT + 1):
                    e0 = 2 * (r - 1)
                    for c in range(CH):
                        if has_tile(g, r):
                            transposes(g, r, c)
                        if has_experts(g):
                            up(g, e0 + c // KH, c % KH)
                        if has_tile(g, r) and c:
                            attend(g, r, c - 1)
                        if has_experts(g) and e0 + c // KH >= 1:
                            down(g, e0 + c // KH - 1, c % KH)
                        if has_tile(g, r - 1):
                            finish(g, r - 1, c)
                    if has_tile(g, r):
                        attend(g, r, CH - 1)
                if has_experts(g):
                    for b in range(GT):
                        down(g, E - 1, b)

            bodies(pe, steps)


_OUT = ((4096, 128), "float32")


def kernel(x, adj, L0_gnn_W_w, L0_gnn_W_b, L0_gnn_a, L0_ffn_Wg, L0_ffn_bg, L0_ffn_W1, L0_ffn_b1,
           L0_ffn_W2, L0_ffn_b2):
    import numpy as np
    import concourse.bacc as bacc
    from concourse import mybir as mb
    from concourse.bass_utils import run_bass_kernel_spmd

    def flat(v):
        return np.ascontiguousarray(v)

    W1, b1, W2 = np.asarray(L0_ffn_W1), np.asarray(L0_ffn_b1), np.asarray(L0_ffn_W2)
    E, HID, F = W1.shape
    arrays = {
        "x": flat(x),
        "adj": flat(adj),
        "W": flat(L0_gnn_W_w),
        "Wb": flat(np.asarray(L0_gnn_W_b).reshape(1, F)),
        "a": flat(L0_gnn_a),
        "WgT": flat(np.asarray(L0_ffn_Wg).T),
        "bg": flat(np.asarray(L0_ffn_bg).reshape(1, E)),
        "w1": flat(W1.transpose(2, 0, 1).reshape(F, E * HID)),
        "b1": flat(b1.reshape(E, HID // 128, 128).transpose(2, 0, 1).reshape(128, -1)),
        "w2": flat(W2.reshape(E, F, HID // 128, 128).transpose(3, 0, 2, 1)),
        "b2": flat(L0_ffn_b2),
    }
    nc = bacc.Bacc("TRN2", target_bir_lowering=False, num_devices=1)
    args = [nc.dram_tensor(k, v.shape, mb.dt.from_np(v.dtype), kind="ExternalInput").ap() for k, v in arrays.items()]
    args.append(nc.dram_tensor("out", _OUT[0], mb.dt.from_np(np.dtype(_OUT[1])), kind="ExternalOutput").ap())
    build(nc, *args)
    r = run_bass_kernel_spmd(nc, [arrays], core_ids=[0])
    return r.results[0]["out"]
```

```python
import concourse.bass as bass
from concourse import mybir
from contextlib import ExitStack


def build(nc, x, adjT, W, Wb, a, WgT, bg, w1, b1, w2, b2, out):
    fp32, fp16, bf16 = mybir.dt.float32, mybir.dt.float16, mybir.dt.bfloat16
    i32, u32 = mybir.dt.int32, mybir.dt.uint32
    ALU = mybir.AluOpType
    ACT = mybir.ActivationFunctionType
    X = mybir.AxisListType.X

    N, F = x.shape
    E = WgT.shape[1]
    HID = w1.shape[1] // E
    P = 128
    TILES = N // P
    GT = 4
    GROUPS = TILES // GT
    GW = GT * P
    KH = HID // P
    CH = 8
    STEPS = TILES // CH
    PAIRS = TILES // 2
    ADJ = 4
    LOADS = TILES // ADJ
    FW = F + 1
    EPS = 1e-5
    SLOPE = 0.2
    WS = 2.0 ** 8
    RANGE = 60.0
    TOP = 60.0
    NFIN = 14
    LAG = 2
    assert E == 2 * GT and KH == 4 and STEPS == GT

    ctx = ExitStack()
    with ctx:
        def sb(name, shape, dt=fp32):
            return ctx.enter_context(nc.sbuf_tensor(name, shape, dt))

        def pb(name, shape=(P, 512)):
            return ctx.enter_context(nc.psum_tensor(name, list(shape), fp32))

        def sem(name):
            return ctx.enter_context(nc.semaphore(name))

        adj_sb = [sb(f"adj{i}", [P, ADJ, GW], i32) for i in range(4)]
        G = [sb(f"G{i}", [P, 2, GW]) for i in range(4)]
        prob = [sb(f"prob{i}", [P, 2, GW]) for i in range(4)]
        Wh = sb("Wh", [P, TILES, FW])
        w1_hi = sb("w1_hi", [P, E * HID], fp16)
        w1_lo = sb("w1_lo", [P, E * HID], fp16)
        w2_hi = sb("w2_hi", [P, E, KH, F], fp16)
        w2_lo = sb("w2_lo", [P, E, KH, F], fp16)
        stage = sb("stage", [P, E * HID])
        adj_pre = [w[:, :].bitcast(i32).rearrange("p (u i) -> p u i", i=GW)
                   for w in (w1_hi, w1_lo)]
        vrun = w2_hi[:, 0:2, :, :].rearrange("p e k f -> p (e k f)").bitcast(fp32)
        vmask = w2_hi[:, 2:4, :, :].rearrange("p e k f -> p (e k f)").bitcast(fp32)
        xin = stage[:, :].rearrange("p (c f) -> p c f", f=F)
        r = [sb(f"r{i}", [P, GW]) for i in range(4)]
        xh = r[0][:, :].rearrange("p (b f) -> p b f", f=F)
        h_hi = [sb(f"h_hi{i}", [P, KH, GW], fp16) for i in range(2)]
        h_lo = [sb(f"h_lo{i}", [P, KH, GW], fp16) for i in range(2)]
        ident = sb("ident", [P, P])
        ones = sb("ones", [P, P])
        W_sb = sb("W_sb", [P, F])
        a_sb = sb("a_sb", [P, 2])
        a1_bc = sb("a1_bc", [P, P])
        Wb_row = sb("Wb_row", [P, F])
        Wb_col = sb("Wb_col", [P, 1])
        WgT_sb = sb("WgT_sb", [P, E])
        bg_bc = sb("bg_bc", [P, E])
        b1_sb = sb("b1_sb", [P, E * KH])
        b2_sb = sb("b2_sb", [E, F])
        lane = sb("lane", [P, E])
        mhalf = sb("mhalf", [P, GT])
        hT = [prob[2][:, i, :] for i in range(2)]
        whT = [prob[3][:, i, :] for i in range(2)]
        t_col = sb("t_col", [P, TILES])
        B_col = sb("B_col", [P, TILES])
        D_col = sb("D_col", [P, TILES])
        tm_p = sb("tm_p", [P, 2])
        tends = sb("tends", [P, 2])
        tmax = tends[:, 0:1]
        tneg = sb("tneg", [P, TILES])
        tmin = sb("tmin", [P, 1])
        narrow = sb("narrow", [P, 1], i32)
        v_col = sb("v_col", [P, TILES])
        m_bc = sb("m_bc", [P, N])
        bB = sb("bB", [P, 1])
        bD = sb("bD", [P, 1])
        bC = sb("bC", [P, 1])
        whsum = sb("whsum", [P, F])
        s_bc = sb("s_bc", [P, N])
        cexp = sb("cexp", [P, GW])
        c_g = sb("c_g", [P, GW])
        hsum8 = sb("hsum8", [P, GROUPS])
        hsum = sb("hsum", [P, 1])
        hsum_bc = sb("hsum_bc", [P, P])
        st = sb("st", [P, GT, 6])
        mv = sb("mv", [P, GT, 2])
        ve = sb("ve", [P, GT])
        rstd = sb("rstd", [P, GT])
        xt = sb("xt", [P, GT, F])
        x1n = sb("x1n", [P, GT, F])
        combn = sb("combn", [P, GT, E])
        yacc, ot, num = (stage[:, i * GW:(i + 1) * GW].rearrange("p (b f) -> p b f", f=F) for i in range(3))
        combc = sb("combc", [P, GT, E])
        xnT = sb("xnT", [P, GW])
        x_hi = sb("x_hi", [P, GW], fp16)
        x_lo = sb("x_lo", [P, GW], fp16)
        xn = sb("xn", [P, GT, F])
        den = sb("den", [P, GT])
        emp = sb("emp", [P, GT])
        den1 = sb("den1", [P, GT])
        rden = sb("rden", [P, GT])
        gs = sb("gs", [P, GT, E])
        m8 = sb("m8", [P, GT, 8])
        ix = sb("ix", [P, GT, 8], u32)
        ixf = sb("ixf", [P, GT, 2])
        gd = sb("gd", [P, GT])
        ed = sb("ed", [P, GT])
        eq = sb("eq", [P, GT])
        p1 = sb("p1", [P, GT])
        p2 = sb("p2", [P, GT])
        c1 = sb("c1", [P, GT, E])
        c2 = sb("c2", [P, GT, E])
        combT = sb("combT", [E, GW])
        idle = sb("idle", [1, 4 + LOADS])

        acc = [pb(f"acc{i}") for i in range(2)]
        hps = [pb(f"hps{i}") for i in range(2)]
        yps = [pb(f"yps{i}") for i in range(2)]
        m1 = pb("m1")
        m2 = pb("m2")

        s_wa = sem("s_wa")
        s_we = sem("s_we")
        s_w1 = sem("s_w1")
        s_w2 = sem("s_w2")
        s_xin = [sem(f"s_xin{i}") for i in range(GROUPS)]
        s_adj = [sem(f"s_adj{i}") for i in range(4)]
        s_xt = sem("s_xt")
        s_zero = sem("s_zero")
        s_const = sem("s_const")
        s_pl = sem("s_pl")
        s_ve = sem("s_ve")
        s_rstd = sem("s_rstd")
        s_xh = sem("s_xh")
        s_t0 = sem("s_t0")
        s_hT = sem("s_hT")
        s_whT = sem("s_whT")
        s_whTs = sem("s_whTs")
        s_wh = sem("s_wh")
        s_whs = sem("s_whs")
        s_ts = sem("s_ts")
        s_tse = sem("s_tse")
        s_sbc = sem("s_sbc")
        s_pre = sem("s_pre")
        s_tm = sem("s_tm")
        s_tmax = sem("s_tmax")
        s_bias0 = sem("s_bias0")
        s_BD = sem("s_BD")
        s_split = sem("s_split")
        s_whm = sem("s_whm")
        s_whx = sem("s_whx")
        s_cexp = sem("s_cexp")
        s_hs = sem("s_hs")
        s_G = sem("s_G")
        s_cg = sem("s_cg")
        s_P = sem("s_P")
        s_at = sem("s_at")
        s_den = sem("s_den")
        s_fin = sem("s_fin")
        s_num = sem("s_num")
        s_x1 = sem("s_x1")
        s_xn = sem("s_xn")
        s_xtp = sem("s_xtp")
        s_xnt = sem("s_xnt")
        s_xhi = sem("s_xhi")
        s_xlo = sem("s_xlo")
        s_gate = sem("s_gate")
        s_gd = sem("s_gd")
        s_ed = sem("s_ed")
        s_comb = sem("s_comb")
        s_ctp = sem("s_ctp")
        s_cT = sem("s_cT")
        s_bias = sem("s_bias")
        s_res = sem("s_res")
        s_cpc = sem("s_cpc")
        s_h = sem("s_h")
        s_r = sem("s_r")
        s_hi = sem("s_hi")
        s_lo = sem("s_lo")
        s_y = sem("s_y")
        s_cb = sem("s_cb")
        s_out = sem("s_out")
        s_narrow = sem("s_narrow")
        s_pre_adj = [sem(f"s_pre_adj{i}") for i in range(2)]
        s_vl = sem("s_vl")
        s_vmax = sem("s_vmax")
        s_wl = sem("s_wl")
        s_w = sem("s_w")

        def ge(eng, s, value):
            if not (isinstance(value, int) and value <= 0):
                eng.wait_ge(s, value)

        def bodies(eng, steps):
            steps(-1)
            steps(0)
            steps(1)
            with eng.Fori(2, GROUPS - 1) as g:
                steps(g)
            steps(GROUPS - 1)
            steps(GROUPS)
            steps(GROUPS + 1)

        def is_group(g):
            return not isinstance(g, int) or 0 <= g < GROUPS

        def unit(g, rr, c):
            if c >= CH:
                rr, c = rr + c // CH, c % CH
            if rr > GT:
                g, rr = g + 1, rr - GT
            return (g + 1, c) if rr == GT else (g, CH * rr + c)

        block = ctx.enter_context(nc.Block())

        @block.sync
        def _(sp):
            xv = x.rearrange("(c p) f -> p c f", p=P)
            for g in range(GROUPS):
                sp.dma_start(xin[:, GT * g:GT * (g + 1), :], xv[:, GT * g:GT * (g + 1), :]).then_inc(s_xin[g], 16)
                if g == 0:
                    sp.dma_start(W_sb[:, :], W).then_inc(s_wa, 16)
                    sp.dma_start(a_sb[:, 0:1], a[0:F, :]).then_inc(s_wa, 16)
                    sp.dma_start(a_sb[:, 1:2], a[F:2 * F, :]).then_inc(s_wa, 16)
                    sp.dma_start(Wb_row[:, :], Wb[0:1, :].broadcast_to([P, F])).then_inc(s_wa, 16)
                    sp.dma_start(Wb_col[:, :], Wb.rearrange("a f -> f a")).then_inc(s_wa, 16)

            def load_adj(g, n):
                if n >= 4 or not (isinstance(g, int) and g == 0):
                    sp.wait_ge(s_P, 2 * (LOADS * g + n - 3))
                sp.dma_start(adj_sb[n % 4][:, :, :],
                             adjT[bass.ds(P * g, P), ADJ * n:ADJ * (n + 1), :]).then_inc(s_adj[n % 4], 16)

            def load_x(g):
                ge(sp, s_x1, g)
                sp.dma_start(xt[:, :, :], x[bass.ds(g * GW, GW), :].rearrange("(c p) f -> p c f", p=P))\
                    .then_inc(s_xt, 16)

            def store_group(n):
                sp.wait_ge(s_cb, E * (n + 1))
                sp.dma_start(out[bass.ds(n * GW, GW), :].rearrange("(c p) f -> p c f", p=P),
                             ot[:, :, :]).then_inc(s_out, 16)

            for n in range(4):
                load_adj(0, n)
            sp.dma_start(WgT_sb[:, :], WgT).then_inc(s_we, 16)
            sp.dma_start(bg_bc[:, :], bg[0:1, :].broadcast_to([P, E])).then_inc(s_we, 16)
            sp.dma_start(b1_sb[:, :], b1).then_inc(s_we, 16)
            sp.dma_start(b2_sb[:, :], b2).then_inc(s_we, 16)
            load_x(0)
            sp.wait_ge(s_xh, GROUPS)
            sp.dma_start(stage[:, :], w1).then_inc(s_w1, 16)
            sp.wait_ge(s_narrow, 1)
            fast = sp.value_load(narrow[0:1, 0:1])
            with sp.If(fast == 0):
                def load_pre(g):
                    for n in range(LOADS):
                        if n >= 2 or not isinstance(g, int):
                            sp.wait_ge(s_vl, 2 + 2 * ADJ * (LOADS * g + n - 1))
                        sp.dma_start(adj_pre[n % 2][:, :, :],
                                     adjT[bass.ds(P * g, P), ADJ * n:ADJ * (n + 1), :]).then_inc(s_pre_adj[n % 2], 16)

                load_pre(0)
                with sp.Fori(1, GROUPS) as g:
                    load_pre(g)
            for n in range(4, LOADS):
                load_adj(0, n)
                if n == 4:
                    sp.wait_ge(s_split, 2)
                    sp.dma_start(stage[:, :], w2.rearrange("p e k f -> p (e k f)")).then_inc(s_w2, 16)
            for g in (1,):
                for n in range(LOADS):
                    load_adj(g, n)
                    if n == 1:
                        load_x(g)
            with sp.Fori(2, GROUPS) as g:
                for n in range(LOADS):
                    load_adj(g, n)
                    if n == 1:
                        load_x(g)
                    if n == 4:
                        store_group(g - 2)
            store_group(GROUPS - 2)
            store_group(GROUPS - 1)
            sp.wait_ge(s_out, 16 * GROUPS)

        @block.gpsimd
        def _(pool):
            nc.gpsimd.memset(ident[:, :], 0.0).then_inc(s_zero, 1)
            nc.gpsimd.memset(mhalf[:, :], -0.5).then_inc(s_const, 1)
            nc.gpsimd.memset(ones[:, :], 1.0).then_inc(s_const, 1)
            nc.gpsimd.iota(lane[:, :], [[1, E]], base=0, channel_multiplier=0,
                           allow_small_or_imprecise_dtypes=True).then_inc(s_const, 1)
            pool.wait_ge(s_zero, 1)
            nc.gpsimd.affine_select(out=ident[:, :], in_=ident[:, :], compare_op=ALU.not_equal, fill=1.0,
                                    base=0, pattern=[[-1, P]], channel_multiplier=1).then_inc(s_const, 1)
            pool.wait_ge(s_const, 4)
            with pool.Fori(0, GROUPS) as g:
                pool.wait_ge(s_ve, g + 1)
                nc.gpsimd.tensor_tensor(rstd[:, :], ve[:, :], mhalf[:, :], ALU.pow).then_inc(s_rstd, 1)
            pool.wait_ge(s_tm, 1)
            nc.gpsimd.partition_all_reduce(tends[:, :], tm_p[:, :], P, bass.bass_isa.ReduceOp.max).then_inc(s_tmax, 1)
            pool.wait_ge(s_narrow, 1)
            fast = pool.value_load(narrow[0:1, 0:1])
            with pool.If(fast == 0):
                for g in range(GROUPS):
                    pool.wait_ge(s_vl, 2 + 2 * TILES * (g + 1))
                    nc.gpsimd.partition_all_reduce(m_bc[:, g * GW:(g + 1) * GW], vrun[:, :], P,
                                                   bass.bass_isa.ReduceOp.max).then_inc(s_vmax, 1)
            with pool.Fori(GROUPS, 2 * GROUPS) as g:
                pool.wait_ge(s_ve, g + 1)
                nc.gpsimd.tensor_tensor(rstd[:, :], ve[:, :], mhalf[:, :], ALU.pow).then_inc(s_rstd, 1)

        @block.vector
        def _(dve):
            links = [0]

            def link(ins):
                links[0] += 1
                ins.then_inc(s_pl, 1)
                dve.wait_ge(s_pl, links[0])

            dve.wait_ge(s_const, 4)
            dve.wait_ge(s_wa, 80)
            nc.vector.tensor_scalar(a1_bc[:, :], ones[:, :], a_sb[:, 0:1], None, ALU.mult).then_inc(s_pre, 1)
            nc.vector.memset(Wh[:, :, F:FW], 1.0).then_inc(s_pre, 1)
            nc.vector.memset(idle[:, 1:2], 0.0).then_inc(s_pre, 1)

            def stats(g):
                dve.wait_ge(s_xin[g], 16)
                for b in range(GT):
                    last = nc.vector.bn_stats(st[:, b, :], xin[:, GT * g + b, :])
                link(last)
                if g >= 1:
                    dve.wait_ge(s_xh, g)
                for b in range(GT):
                    last = nc.vector.bn_aggr(mv[:, b, :], st[:, b, :])
                link(last)
                nc.vector.tensor_scalar(ve[:, :], mv[:, :, 1], EPS, None, ALU.add).then_inc(s_ve, 1)

            def normalise(g):
                dve.wait_ge(s_rstd, g + 1)
                if g >= 1:
                    dve.wait_ge(s_t0, g)
                for b in range(GT):
                    ins = nc.vector.tensor_scalar(xh[:, b, :], xin[:, GT * g + b, :], mv[:, b, 0:1],
                                                  rstd[:, b:b + 1], ALU.subtract, ALU.mult)
                ins.then_inc(s_xh, 1)

            def keep_Wh(g):
                dve.wait_ge(s_wh, g + 1)
                for b in range(GT):
                    last = nc.vector.tensor_tensor(Wh[:, GT * g + b, 0:F], yps[g % 2][:, b * P:(b + 1) * P],
                                                   Wb_row[:, :], ALU.add)
                last.then_inc(s_whs, 1)

            for i in range(GROUPS + 2):
                if i < GROUPS:
                    stats(i)
                    normalise(i)
                if i >= 2:
                    keep_Wh(i - 2)
            dve.wait_ge(s_ts, GROUPS)
            nc.vector.tensor_copy(t_col[:, :], m2[:, 0:TILES])
            nc.vector.tensor_scalar(tneg[:, :], m2[:, 0:TILES], -1.0, None, ALU.mult).then_inc(s_tse, 1)
            dve.wait_ge(s_tse, 1)
            nc.vector.tensor_reduce(tm_p[:, 0:1], t_col[:, :], X, ALU.max)
            nc.vector.tensor_reduce(tm_p[:, 1:2], tneg[:, :], X, ALU.max).then_inc(s_tm, 1)
            dve.wait_ge(s_hT, GROUPS)
            link(nc.vector.tensor_reduce(hsum[:, :], hsum8[:, :], X, ALU.add))
            nc.vector.tensor_scalar(hsum_bc[:, :], ones[:, :], hsum[:, :], None, ALU.mult).then_inc(s_hs, 1)
            dve.wait_ge(s_tmax, 1)
            nc.vector.tensor_scalar(bB[:, :], tmax, -1.0, None, ALU.mult)
            nc.vector.tensor_scalar(bD[:, :], tmax, -SLOPE, None, ALU.mult)
            nc.vector.tensor_scalar(bC[:, :], tmax, -(1.0 - SLOPE), None, ALU.mult).then_inc(s_bias0, 1)
            link(nc.vector.tensor_tensor(tmin[:, :], tends[:, 0:1], tends[:, 1:2], ALU.add))
            nc.vector.tensor_scalar(narrow[:, :], tmin[:, :], RANGE, None, ALU.is_le).then_inc(s_narrow, 1)
            dve.wait_ge(s_whx, 1)
            nc.vector.scalar_tensor_tensor(whsum[:, :], Wb_row[:, :], float(N), m1[:, 0:F], op0=ALU.mult,
                                           op1=ALU.add).then_inc(s_whm, 1)

            def group_row(g):
                dve.wait_ge(s_cexp, g + 1)
                ge(dve, s_G, PAIRS * g)
                nc.vector.tensor_scalar(c_g[:, :], cexp[:, :], 1.0, None, ALU.min).then_inc(s_cg, 1)

            def row_maxima():
                dve.wait_ge(s_narrow, 1)
                nc.vector.tensor_scalar(tmin[:, :], tends[:, 1:2], -1.0, None, ALU.mult).then_inc(s_vl, 1)
                dve.wait_ge(s_vl, 1)
                nc.vector.tensor_scalar(v_col[:, :], t_col[:, :], tmin[:, :], None, ALU.subtract).then_inc(s_vl, 1)
                dve.wait_ge(s_vl, 2)
                with dve.Fori(0, GROUPS) as g:
                    for u in range(TILES):
                        n = 2 + 2 * TILES * g + 2 * u
                        if u % ADJ == 0:
                            k = u // ADJ
                            dve.wait_ge(s_pre_adj[k % 2], 16 * (LOADS // 2 * g + k // 2 + 1))
                        dve.wait_ge(s_vl, n)
                        nc.vector.tensor_scalar(vmask[:, :], adj_pre[u // ADJ % 2][:, u % ADJ, :], 0.0,
                                                v_col[:, u:u + 1], ALU.is_gt, ALU.mult).then_inc(s_vl, 1)
                        dve.wait_ge(s_vl, n + 1)
                        if u == 0:
                            nc.vector.tensor_copy(vrun[:, :], vmask[:, :]).then_inc(s_vl, 1)
                        else:
                            nc.vector.tensor_tensor(vrun[:, :], vrun[:, :], vmask[:, :], ALU.max).then_inc(s_vl, 1)
                    dve.wait_ge(s_vmax, g + 1)
                n = 2 + 2 * TILES * GROUPS
                nc.vector.scalar_tensor_tensor(m_bc[:, :], m_bc[:, :], tmin[:, :], s_bc[:, :], op0=ALU.add,
                                               op1=ALU.add).then_inc(s_vl, 1)
                dve.wait_ge(s_vl, n + 1)
                nc.vector.scalar_tensor_tensor(m_bc[:, :], m_bc[:, :], SLOPE, m_bc[:, :], op0=ALU.mult,
                                               op1=ALU.max).then_inc(s_vl, 1)
                dve.wait_ge(s_vl, n + 2)

            def make_logits(g, rr, c):
                g, u = unit(g, rr, c)
                if not is_group(g):
                    return
                n = PAIRS * g + u // 2
                Gp = G[u // 2 % 4]
                ge(dve, s_P, n - 3)
                for k in range(2):
                    last = nc.vector.tensor_scalar(Gp[:, k, :], s_bc[:, bass.ds(g * GW, GW)], t_col[:, u + k:u + k + 1],
                                                   None, ALU.add)
                last.then_inc(s_wl, 1)
                dve.wait_ge(s_wl, 3 * n + 1)
                nc.vector.scalar_tensor_tensor(Gp[:, :, :], Gp[:, :, :], SLOPE, Gp[:, :, :], op0=ALU.mult,
                                               op1=ALU.max).then_inc(s_wl, 1)
                dve.wait_ge(s_wl, 3 * n + 2)
                for k in range(2):
                    last = nc.vector.tensor_tensor(Gp[:, k, :], Gp[:, k, :], m_bc[:, bass.ds(g * GW, GW)], ALU.subtract)
                last.then_inc(s_wl, 1)
                dve.wait_ge(s_wl, 3 * n + 3)
                nc.vector.tensor_scalar(Gp[:, :, :], Gp[:, :, :], TOP, None, ALU.min).then_inc(s_w, 1)

            def make_G(g, rr, c):
                g, u = unit(g, rr, c)
                if not is_group(g):
                    return
                n = PAIRS * g + u // 2
                if u == 0:
                    group_row(g)
                    dve.wait_ge(s_cg, g + 1)
                ge(dve, s_P, n - 3)
                for k in range(2):
                    last = nc.vector.tensor_scalar(G[u // 2 % 4][:, k, :], c_g[:, :], D_col[:, u + k:u + k + 1],
                                                   B_col[:, u + k:u + k + 1], ALU.mult, ALU.max)
                last.then_inc(s_G, 1)

            def make_P(g, rr, c):
                g, u = unit(g, rr, c)
                if not is_group(g):
                    return
                n = PAIRS * g + u // 2
                k = u // ADJ
                if u % ADJ == 0:
                    dve.wait_ge(s_adj[k % 4], 16 * (LOADS // 4 * g + k // 4 + 1))
                dve.wait_ge(s_G, n + 1)
                ge(dve, s_at, 2 * (n - 3))
                nc.vector.scalar_tensor_tensor(prob[u // 2 % 4][:, :, :], adj_sb[k % 4][:, u % ADJ:u % ADJ + 2, :],
                                               0.0, G[u // 2 % 4][:, :, :], op0=ALU.is_gt,
                                               op1=ALU.mult).then_inc(s_P, 1)

            def low_part(g, e, k):
                n = KH * (E * (g - 1) + e) + k
                dve.wait_ge(s_hi, n + 1)
                if k == 0:
                    ge(dve, s_y, E * (g - 1) + e - 1)
                nc.vector.tensor_tensor(h_lo[e % 2][:, k, :], r[k][:, :], h_hi[e % 2][:, k, :],
                                        ALU.subtract).then_inc(s_lo, 1)

            def combine(g, e):
                n = E * (g - 1) + e
                dve.wait_ge(s_y, n + 1)
                ge(dve, s_cb, n)
                if e == 0:
                    dve.wait_ge(s_cpc, g)
                if e == E - 1:
                    ge(dve, s_out, 16 * (g - 1))
                dst = ot if e == E - 1 else yacc
                for b in range(GT):
                    last = nc.vector.scalar_tensor_tensor(
                        dst[:, b, :], yps[e % 2][:, b * P:(b + 1) * P], combc[:, b, e:e + 1],
                        yacc[:, b, :], op0=ALU.mult, op1=ALU.add)
                last.then_inc(s_cb, 1)

            def hand_over(g):
                dve.wait_ge(s_res, g + 1)
                dve.wait_ge(s_comb, g + 1)
                dve.wait_ge(s_split, 4)
                ge(dve, s_cb, E * g)
                nc.vector.tensor_copy(yacc[:, :, :], x1n[:, :, :])
                nc.vector.tensor_scalar(combc[:, :, :], combn[:, :, :], 1.0 / WS, None, ALU.mult).then_inc(s_cpc, 1)

            def bc(ap, n):
                return ap.unsqueeze(2).broadcast_to([P, GT, n])

            def finish(g, part):
                def after(k):
                    dve.wait_ge(s_fin, NFIN * g + k)

                if part == 1:
                    dve.wait_ge(s_split, 4)
                    dve.wait_ge(s_at, TILES * (g + 1))
                    for i in range(2):
                        ins = nc.vector.tensor_copy(den[:, 2 * i:2 * i + 2], acc[i][:, F:F + FW + 1:FW])
                    ins.then_inc(s_fin, 1)
                    after(1)
                    nc.vector.tensor_scalar(emp[:, :], den[:, :], 0.0, None, ALU.is_equal).then_inc(s_fin, 1)
                    after(2)
                    nc.vector.scalar_tensor_tensor(den1[:, :], emp[:, :], float(N), den[:, :], op0=ALU.mult,
                                                   op1=ALU.add).then_inc(s_fin, 1)
                    for b in range(GT):
                        ins = nc.vector.scalar_tensor_tensor(
                            num[:, b, :], whsum[:, :], emp[:, b:b + 1], acc[b // 2][:, b % 2 * FW:b % 2 * FW + F],
                            op0=ALU.mult, op1=ALU.add)
                    ins.then_inc(s_num, 1)
                    after(3)
                    nc.vector.reciprocal(rden[:, :], den1[:, :]).then_inc(s_fin, 1)
                    after(4)
                    dve.wait_ge(s_num, g + 1)
                    dve.wait_ge(s_xt, 16 * (g + 1))
                    for b in range(GT):
                        ins = nc.vector.scalar_tensor_tensor(x1n[:, b, :], num[:, b, :], rden[:, b:b + 1],
                                                             xt[:, b, :], op0=ALU.mult, op1=ALU.add)
                    ins.then_inc(s_x1, 1)
                if part == 2:
                    dve.wait_ge(s_x1, g + 1)
                    for b in range(GT):
                        ins = nc.vector.bn_stats(st[:, b, :], x1n[:, b, :])
                    ins.then_inc(s_fin, 1)
                    after(5)
                    nc.vector.memset(idle[:, 3:4], 0.0)
                    for b in range(GT):
                        ins = nc.vector.bn_aggr(mv[:, b, :], st[:, b, :])
                    ins.then_inc(s_fin, 1)
                    after(6)
                    nc.vector.tensor_scalar(ve[:, :], mv[:, :, 1], EPS, None, ALU.add).then_inc(s_ve, 1)
                if part == 3:
                    dve.wait_ge(s_rstd, GROUPS + g + 1)
                    ge(dve, s_xtp, g)
                    for b in range(GT):
                        ins = nc.vector.tensor_scalar(xn[:, b, :], x1n[:, b, :], mv[:, b, 0:1], rstd[:, b:b + 1],
                                                      ALU.subtract, ALU.mult)
                    ins.then_inc(s_xn, 1)
                if part == 6:
                    dve.wait_ge(s_gate, g + 1)
                    nc.vector.tensor_tensor(gs[:, :, :], m2[:, 0:GT * E].rearrange("p (b e) -> p b e", e=E),
                                            bg_bc[:, :].unsqueeze(1).broadcast_to([P, GT, E]),
                                            ALU.add).then_inc(s_fin, 1)
                    after(7)
                    nc.vector.memset(idle[:, 3:4], 0.0)
                    for b in range(GT):
                        ins = nc.vector.max(m8[:, b, :], gs[:, b, :])
                    ins.then_inc(s_fin, 1)
                    after(8)
                    nc.vector.tensor_tensor(gd[:, :], m8[:, :, 1], m8[:, :, 0], ALU.subtract).then_inc(s_gd, 1)
                    for b in range(GT):
                        ins = nc.vector.max_index(ix[:, b, :], m8[:, b, :], gs[:, b, :])
                    ins.then_inc(s_fin, 1)
                    after(9)
                    nc.vector.tensor_copy(ixf[:, :, :], ix[:, :, 0:2]).then_inc(s_fin, 1)
                if part == 7:
                    dve.wait_ge(s_ed, g + 1)
                    nc.vector.tensor_scalar(eq[:, :], ed[:, :], 1.0, None, ALU.add).then_inc(s_fin, 1)
                    after(11)
                    nc.vector.reciprocal(p1[:, :], eq[:, :]).then_inc(s_fin, 1)
                    after(12)
                    nc.vector.tensor_tensor(p2[:, :], ed[:, :], p1[:, :], ALU.mult).then_inc(s_fin, 1)
                    after(13)
                    for b in range(GT):
                        nc.vector.tensor_scalar(c1[:, b, :], lane[:, :], ixf[:, b, 0:1], p1[:, b:b + 1],
                                                ALU.is_equal, ALU.mult)
                    for b in range(GT):
                        ins = nc.vector.tensor_scalar(c2[:, b, :], lane[:, :], ixf[:, b, 1:2], p2[:, b:b + 1],
                                                      ALU.is_equal, ALU.mult)
                    ins.then_inc(s_fin, 1)
                    after(14)
                    nc.vector.tensor_tensor(combn[:, :, :], c1[:, :, :], c2[:, :, :], ALU.add).then_inc(s_comb, 1)

            def residual(g):
                dve.wait_ge(s_bias, g + 1)
                nc.vector.tensor_tensor(x1n[:, :, :], x1n[:, :, :],
                                        m1[:, :].rearrange("p (b f) -> p b f", f=F), ALU.add).then_inc(s_res, 1)

            def split(hi, lo, src):
                link(nc.vector.tensor_scalar(hi, src, WS, None, ALU.mult))
                nc.vector.scalar_tensor_tensor(lo, src, WS, hi, op0=ALU.mult, op1=ALU.subtract).then_inc(s_split, 2)

            def steps(g, weigh):
                ffn = not isinstance(g, int) or 1 <= g <= GROUPS
                for rr in range(1, GT + 1):
                    e0 = 2 * (rr - 1)
                    for c in range(CH):
                        if c % 2 == 0:
                            weigh(g, rr, c + 4)
                            make_P(g, rr, c + 2)
                        if ffn and (c >= LAG or rr > 1):
                            e, k = divmod(KH * e0 + c - LAG, KH)
                            low_part(g, e, k)
                        if rr == 1:
                            if is_group(g - 1) and c == 0:
                                residual(g - 1)
                            if is_group(g - 2) and c in (1, 3):
                                combine(g - 1, E - 2 + c // 2)
                            if is_group(g - 1) and c == 4:
                                hand_over(g - 1)
                        elif ffn and c in (1, 5):
                            combine(g, e0 - 2 + c // 4)
                        if is_group(g) and rr == GT:
                            finish(g, c)
                    if isinstance(g, int) and g == 0 and rr == 1:
                        dve.wait_ge(s_w1, 16)
                        split(w1_hi[:, :], w1_lo[:, :], stage[:, :])
                    if isinstance(g, int) and g == 0 and rr == 3:
                        dve.wait_ge(s_w2, 16)
                        split(w2_hi[:, :, :, :].rearrange("p e k f -> p (e k f)"),
                              w2_lo[:, :, :, :].rearrange("p e k f -> p (e k f)"), stage[:, :])
                if ffn:
                    for k in range(KH - LAG, KH):
                        low_part(g, E - 1, k)
                if is_group(g):
                    dve.wait_ge(s_xhi, g + 1)
                    nc.vector.tensor_tensor(x_lo[:, :], xnT[:, :], x_hi[:, :], ALU.subtract).then_inc(s_xlo, 1)

            def program(weigh):
                weigh(-1, GT, 0)
                weigh(-1, GT, 2)
                make_P(-1, GT, 0)

                def schedule(g):
                    if isinstance(g, int) and g == -1:
                        for c in range(0, CH, 2):
                            weigh(g, GT, c + 4)
                            make_P(g, GT, c + 2)
                    else:
                        steps(g, weigh)

                bodies(dve, schedule)

            dve.wait_ge(s_narrow, 1)
            fast = dve.value_load(narrow[0:1, 0:1])
            dve.wait_ge(s_BD, 2)
            before = links[0]
            with dve.If(fast != 0):
                program(make_G)
            with dve.Else():
                links[0] = before
                row_maxima()
                program(make_logits)

        @block.scalar
        def _(act):
            act.wait_ge(s_wa, 80)
            for i in range(GROUPS + 2):
                if i < GROUPS:
                    act.wait_ge(s_t0, i + 1)
                    if i >= 2:
                        act.wait_ge(s_wh, i - 1)
                    nc.scalar.activation(hT[i % 2], hps[i % 2][:, :], ACT.Copy,
                                         accum_out=hsum8[:, i:i + 1]).then_inc(s_hT, 1)
                if 1 <= i <= GROUPS:
                    g = i - 1
                    act.wait_ge(s_whT, g + 1)
                    if g >= 2:
                        act.wait_ge(s_ts, g - 1)
                    nc.scalar.activation(whT[g % 2], m1[:, :], ACT.Identity,
                                         bias=Wb_col[:, :]).then_inc(s_whTs, 1)
                if i >= 2:
                    g = i - 2
                    act.wait_ge(s_ts, g + 1)
                    nc.scalar.activation(s_bc[:, g * GW:(g + 1) * GW], acc[g % 2][:, :], ACT.Copy).then_inc(s_sbc, 1)
            act.wait_ge(s_bias0, 1)
            nc.scalar.activation(B_col[:, :], t_col[:, :], ACT.Exp, bias=bB[:, :]).then_inc(s_BD, 1)
            nc.scalar.activation(D_col[:, :], t_col[:, :], ACT.Exp, bias=bD[:, :], scale=SLOPE).then_inc(s_BD, 1)
            act.wait_ge(s_sbc, GROUPS)

            def group_row(g):
                ge(act, s_cg, g)
                nc.scalar.activation(idle[:, 0:1], idle[:, 1:2], ACT.Copy)
                nc.scalar.activation(cexp[:, :], s_bc[:, bass.ds(g * GW, GW)], ACT.Exp, bias=bC[:, :],
                                     scale=-(1.0 - SLOPE)).then_inc(s_cexp, 1)

            def raise_pair(g, rr, c):
                g, u = unit(g, rr, c)
                if not is_group(g):
                    return
                act.wait_ge(s_w, PAIRS * g + u // 2 + 1)
                nc.scalar.activation(G[u // 2 % 4][:, :, :], G[u // 2 % 4][:, :, :], ACT.Exp).then_inc(s_G, 1)

            def relu(g, e, k):
                n = KH * (E * (g - 1) + e) + k
                act.wait_ge(s_h, n + 1)
                ge(act, s_lo, n - KH + 1)
                nc.scalar.activation(r[k][:, :], hps[k % 2][:, :], ACT.Relu, scale=1.0 / WS,
                                     bias=b1_sb[:, KH * e + k:KH * e + k + 1]).then_inc(s_r, 1)

            def high_part(g, e, k):
                n = KH * (E * (g - 1) + e) + k
                act.wait_ge(s_r, n + 1)
                if k == 0:
                    ge(act, s_y, E * (g - 1) + e - 1)
                nc.scalar.activation(h_hi[e % 2][:, k, :], r[k][:, :], ACT.Copy).then_inc(s_hi, 1)

            def finish(g, part):
                if part == 4:
                    act.wait_ge(s_xtp, g + 1)
                    ge(act, s_xlo, g)
                    nc.scalar.activation(xnT[:, :], m1[:, :], ACT.Copy).then_inc(s_xnt, 1)
                if part == 6:
                    act.wait_ge(s_gd, g + 1)
                    nc.scalar.activation(ed[:, :], gd[:, :], ACT.Exp).then_inc(s_ed, 1)
                if part == 7:
                    act.wait_ge(s_ctp, g + 1)
                    nc.scalar.activation(combT[:, :], m2[0:E, :], ACT.Copy).then_inc(s_cT, 1)

            def steps(g, general):
                ffn = not isinstance(g, int) or 1 <= g <= GROUPS
                for rr in range(1, GT + 1):
                    e0 = 2 * (rr - 1)
                    for c in range(CH):
                        if general and c % 2 == 0 and (rr == GT or not isinstance(g, int) or g >= 0):
                            raise_pair(g, rr, c + 4)
                        if ffn:
                            relu(g, e0 + c // KH, c % KH)
                        if ffn:
                            high_part(g, e0 + c // KH, c % KH)
                        if is_group(g) and rr == GT:
                            finish(g, c)
                    if not general and rr == 2 and is_group(g + 1):
                        group_row(g + 1)
                if is_group(g):
                    act.wait_ge(s_xnt, g + 1)
                    ge(act, s_h, KH * E * g)
                    nc.scalar.activation(x_hi[:, :], xnT[:, :], ACT.Copy).then_inc(s_xhi, 1)

            act.wait_ge(s_narrow, 1)
            fast = act.value_load(narrow[0:1, 0:1])
            with act.If(fast != 0):
                bodies(act, lambda g: steps(g, False))
            with act.Else():
                raise_pair(-1, GT, 0)
                raise_pair(-1, GT, 2)
                bodies(act, lambda g: steps(g, True))


        @block.tensor
        def _(pe):
            pe.wait_ge(s_const, 4)
            pe.wait_ge(s_wa, 80)
            pe.wait_ge(s_pre, 3)
            for i in range(GROUPS + 2):
                if i < GROUPS:
                    pe.wait_ge(s_xh, i + 1)
                    if i >= 2:
                        pe.wait_ge(s_hT, i - 1)
                    for b in range(GT):
                        last = nc.tensor.transpose(hps[i % 2][:, b * P:(b + 1) * P], xh[:, b, :], ident[:, :])
                    last.then_inc(s_t0, 1)
                if 1 <= i <= GROUPS:
                    g = i - 1
                    pe.wait_ge(s_hT, g + 1)
                    if g >= 1:
                        pe.wait_ge(s_whTs, g)
                    nc.tensor.matmul(m1[:, :], W_sb[:, :], hT[g % 2], start=True, stop=True).then_inc(s_whT, 1)
                    if g >= 2:
                        pe.wait_ge(s_whs, g - 1)
                    for b in range(GT):
                        last = nc.tensor.matmul(yps[g % 2][:, b * P:(b + 1) * P], hT[g % 2][:, b * P:(b + 1) * P],
                                                W_sb[:, :], start=True, stop=True)
                    last.then_inc(s_wh, 1)
                if i >= 2:
                    g = i - 2
                    pe.wait_ge(s_whTs, g + 1)
                    if g >= 2:
                        pe.wait_ge(s_sbc, g - 1)
                    nc.tensor.matmul(acc[g % 2][:, :], a1_bc[:, :], whT[g % 2], start=True, stop=True)
                    for b in range(GT):
                        last = nc.tensor.matmul(m2[:, GT * g + b:GT * g + b + 1], whT[g % 2][:, b * P:(b + 1) * P],
                                                a_sb[:, 1:2], start=True, stop=True)
                    last.then_inc(s_ts, 1)
            pe.wait_ge(s_hs, 1)
            nc.tensor.matmul(m1[:, 0:F], hsum_bc[:, :], W_sb[:, :], start=True, stop=True).then_inc(s_whx, 1)
            pe.wait_ge(s_sbc, GROUPS)
            pe.wait_ge(s_whs, GROUPS)
            pe.wait_ge(s_we, 64)
            pe.wait_ge(s_tse, 1)

            def attend(g, rr, c):
                g, u = unit(g, rr, c)
                if not is_group(g):
                    return
                n = PAIRS * g + u // 2
                if u == 0:
                    ge(pe, s_num, g)
                if u % 2 == 0:
                    pe.wait_ge(s_P, n + 1)
                for b in range(GT):
                    last = nc.tensor.matmul(acc[b // 2][:, b % 2 * FW:b % 2 * FW + FW],
                                            prob[u // 2 % 4][:, u % 2, b * P:(b + 1) * P], Wh[:, u, :],
                                            start=(u == 0 and b % 2 == 0), stop=(u == TILES - 1),
                                            skip_group_check=True)
                last.then_inc(s_at, 1)

            def up(g, e, k):
                n = KH * (E * (g - 1) + e) + k
                if e == 0 and k == 0:
                    pe.wait_ge(s_xlo, g)
                ge(pe, s_r, n - 1)
                j = e * HID + k * P
                nc.tensor.matmul(hps[k % 2][:, :], w1_hi[:, j:j + P], x_hi[:, :], start=True, stop=False)
                nc.tensor.matmul(hps[k % 2][:, :], w1_hi[:, j:j + P], x_lo[:, :], start=False, stop=False)
                nc.tensor.matmul(hps[k % 2][:, :], w1_lo[:, j:j + P], x_hi[:, :], start=False,
                                 stop=True).then_inc(s_h, 1)

            def down(g, e, b):
                n = E * (g - 1) + e
                if b == 0:
                    pe.wait_ge(s_lo, KH * (n + 1))
                    ge(pe, s_cb, n - 1)
                dst = yps[e % 2][:, b * P:(b + 1) * P]
                for k in range(KH):
                    hi, lo = (v[e % 2][:, k, b * P:(b + 1) * P] for v in (h_hi, h_lo))
                    nc.tensor.matmul(dst, hi, w2_hi[:, e, k, :], start=(k == 0), stop=False)
                    nc.tensor.matmul(dst, hi, w2_lo[:, e, k, :], start=False, stop=False)
                    last = nc.tensor.matmul(dst, lo, w2_hi[:, e, k, :], start=False, stop=(k == KH - 1))
                if b == GT - 1:
                    last.then_inc(s_y, 1)

            def finish(g, part):
                if part == 4:
                    pe.wait_ge(s_xn, g + 1)
                    if isinstance(g, int) and g == 0:
                        pe.wait_ge(s_whm, 1)
                    ge(pe, s_res, g)
                    for b in range(GT):
                        last = nc.tensor.transpose(m1[:, b * P:(b + 1) * P], xn[:, b, :], ident[:, :])
                    last.then_inc(s_xtp, 1)
                if part == 5:
                    pe.wait_ge(s_xnt, g + 1)
                    ge(pe, s_cT, g)
                    for b in range(GT):
                        last = nc.tensor.matmul(m2[:, b * E:(b + 1) * E], xnT[:, b * P:(b + 1) * P], WgT_sb[:, :],
                                                start=True, stop=True)
                    last.then_inc(s_gate, 1)
                if part == CH:
                    pe.wait_ge(s_comb, g + 1)
                    for b in range(GT):
                        last = nc.tensor.transpose(m2[0:E, b * P:(b + 1) * P], combn[:, b, :], ident[:, :])
                    last.then_inc(s_ctp, 1)
                if part == CH + 1:
                    pe.wait_ge(s_cT, g + 1)
                    for b in range(GT):
                        last = nc.tensor.matmul(m1[:, b * P:(b + 1) * P], combT[:, b * P:(b + 1) * P], b2_sb[:, :],
                                                start=True, stop=True)
                    last.then_inc(s_bias, 1)

            def steps(g):
                ffn = not isinstance(g, int) or 1 <= g <= GROUPS
                for rr in range(1, GT + 1):
                    e0 = 2 * (rr - 1)
                    for c in range(CH):
                        if ffn:
                            up(g, e0 + c // KH, c % KH)
                        if rr < GT and not (isinstance(g, int) and g < 0):
                            attend(g, rr, c)
                        if rr == GT:
                            for cc in {0: (), 1: (0,), 2: (1, 2)}.get(c, (c,)):
                                attend(g, rr, cc)
                        if ffn and e0 + c // KH >= 1:
                            down(g, e0 + c // KH - 1, c % KH)
                        if is_group(g) and rr == GT:
                            finish(g, c)
                if is_group(g):
                    finish(g, CH)
                if ffn:
                    for b in range(GT):
                        down(g, E - 1, b)
                if is_group(g):
                    finish(g, CH + 1)

            bodies(pe, steps)


_OUT = ((4096, 128), "float32")


def kernel(x, adj, L0_gnn_W_w, L0_gnn_W_b, L0_gnn_a, L0_ffn_Wg, L0_ffn_bg, L0_ffn_W1, L0_ffn_b1,
           L0_ffn_W2, L0_ffn_b2):
    import numpy as np
    import concourse.bacc as bacc
    from concourse import mybir as mb
    from concourse.bass_utils import run_bass_kernel_spmd

    def flat(v):
        return np.ascontiguousarray(v)

    W1, b1, W2 = np.asarray(L0_ffn_W1), np.asarray(L0_ffn_b1), np.asarray(L0_ffn_W2)
    E, HID, F = W1.shape
    N = np.asarray(x).shape[0]
    arrays = {
        "x": flat(x),
        "adjT": flat(np.asarray(adj).reshape(N // 512, 512, N // 128, 128).transpose(0, 3, 2, 1)
                     .reshape(N // 4, N // 128, 512)),
        "W": flat(L0_gnn_W_w),
        "Wb": flat(np.asarray(L0_gnn_W_b).reshape(1, F)),
        "a": flat(L0_gnn_a),
        "WgT": flat(np.asarray(L0_ffn_Wg).T),
        "bg": flat(np.asarray(L0_ffn_bg).reshape(1, E)),
        "w1": flat(W1.transpose(2, 0, 1).reshape(F, E * HID)),
        "b1": flat(b1.reshape(E, HID // 128, 128).transpose(2, 0, 1).reshape(128, -1)),
        "w2": flat(W2.reshape(E, F, HID // 128, 128).transpose(3, 0, 2, 1)),
        "b2": flat(L0_ffn_b2),
    }
    nc = bacc.Bacc("TRN2", target_bir_lowering=False, num_devices=1)
    args = [nc.dram_tensor(k, v.shape, mb.dt.from_np(v.dtype), kind="ExternalInput").ap() for k, v in arrays.items()]
    args.append(nc.dram_tensor("out", _OUT[0], mb.dt.from_np(np.dtype(_OUT[1])), kind="ExternalOutput").ap())
    build(nc, *args)
    r = run_bass_kernel_spmd(nc, [arrays], core_ids=[0])
    return r.results[0]["out"]
```

```python
import concourse.bass as bass
from concourse import mybir
from contextlib import ExitStack


def build(nc, x, adjT, W, Wb, a, WgT, bg, w1, b1, w2, b2, out):
    fp32, fp16, bf16 = mybir.dt.float32, mybir.dt.float16, mybir.dt.bfloat16
    i32, u32 = mybir.dt.int32, mybir.dt.uint32
    ALU = mybir.AluOpType
    ACT = mybir.ActivationFunctionType
    X = mybir.AxisListType.X

    N, F = x.shape
    E = WgT.shape[1]
    HID = w1.shape[1] // E
    P = 128
    TILES = N // P
    GT = 4
    GROUPS = TILES // GT
    GW = GT * P
    KH = HID // P
    CH = 8
    STEPS = TILES // CH
    PAIRS = TILES // 2
    ADJ = 4
    LOADS = TILES // ADJ
    FW = F + 1
    EPS = 1e-5
    SLOPE = 0.2
    WS = 2.0 ** 8
    RANGE = 60.0
    TOP = 60.0
    NFIN = 14
    LAG = 3
    assert E == 2 * GT and KH == 4 and STEPS == GT

    ctx = ExitStack()
    with ctx:
        def sb(name, shape, dt=fp32):
            return ctx.enter_context(nc.sbuf_tensor(name, shape, dt))

        def pb(name, shape=(P, 512)):
            return ctx.enter_context(nc.psum_tensor(name, list(shape), fp32))

        def sem(name):
            return ctx.enter_context(nc.semaphore(name))

        adj_sb = [sb(f"adj{i}", [P, ADJ, GW], i32) for i in range(4)]
        G = [sb(f"G{i}", [P, 2, GW]) for i in range(4)]
        prob = [sb(f"prob{i}", [P, 2, GW]) for i in range(4)]
        Wh = sb("Wh", [P, TILES, FW])
        w1_hi = sb("w1_hi", [P, E * HID], fp16)
        w1_lo = sb("w1_lo", [P, E * HID], fp16)
        w2_hi = sb("w2_hi", [P, E, KH, F], fp16)
        w2_lo = sb("w2_lo", [P, E, KH, F], fp16)
        stage = sb("stage", [P, E * HID])
        adj_pre = [w[:, :].bitcast(i32).rearrange("p (u i) -> p u i", i=GW)
                   for w in (w1_hi, w1_lo)]
        vrun = w2_hi[:, 0:2, :, :].rearrange("p e k f -> p (e k f)").bitcast(fp32)
        vmask = w2_hi[:, 2:4, :, :].rearrange("p e k f -> p (e k f)").bitcast(fp32)
        xin = stage[:, :].rearrange("p (c f) -> p c f", f=F)
        r = [sb(f"r{i}", [P, GW]) for i in range(4)]
        xh = [r[i][:, :].rearrange("p (b f) -> p b f", f=F) for i in range(2)]
        early = G[3][:, :, :].rearrange("p k i -> p (k i)")
        st0 = early[:, 0:6 * TILES].rearrange("p (u k) -> p u k", k=6)
        mv0 = early[:, 6 * TILES:8 * TILES].rearrange("p (u k) -> p u k", k=2)
        ve0 = early[:, 8 * TILES:9 * TILES]
        rs0 = early[:, 9 * TILES:10 * TILES]
        h_hi = [sb(f"h_hi{i}", [P, KH, GW], fp16) for i in range(2)]
        h_lo = [sb(f"h_lo{i}", [P, KH, GW], fp16) for i in range(2)]
        ident = sb("ident", [P, P])
        ones = sb("ones", [P, P])
        W_sb = sb("W_sb", [P, F])
        a_sb = sb("a_sb", [P, 2])
        wa1_bc = sb("wa1_bc", [P, P])
        Wb_row = sb("Wb_row", [P, F])
        Wb_col = sb("Wb_col", [P, 1])
        WgT_sb = sb("WgT_sb", [P, E])
        bg_bc = sb("bg_bc", [P, E])
        b1_sb = sb("b1_sb", [P, E * KH])
        b2_sb = sb("b2_sb", [E, F])
        lane = sb("lane", [P, E])
        mhalf = sb("mhalf", [P, GT])
        hT = [prob[2][:, i, :] for i in range(2)]
        WT = prob[3][:, 0, 0:P]
        a12_bc = prob[3][:, 1, 0:P]
        wa = sb("wa", [P, 3])
        t_col = sb("t_col", [P, TILES])
        E_col = sb("E_col", [P, TILES])
        D_col = sb("D_col", [P, TILES])
        tm_p = sb("tm_p", [P, 2])
        tends = sb("tends", [P, 2])
        tmax = tends[:, 0:1]
        tneg = sb("tneg", [P, TILES])
        tmin = sb("tmin", [P, 1])
        narrow = sb("narrow", [P, 1], i32)
        v_col = sb("v_col", [P, TILES])
        m_bc = sb("m_bc", [P, N])
        bE = sb("bE", [P, 1])
        bD = sb("bD", [P, 1])
        bC = sb("bC", [P, 1])
        whsum = sb("whsum", [P, F])
        s_bc = sb("s_bc", [P, N])
        cexp = sb("cexp", [P, GW])
        c_g = sb("c_g", [P, GW])
        hsum8 = sb("hsum8", [P, GROUPS])
        hsum = sb("hsum", [P, 1])
        hsum_bc = sb("hsum_bc", [P, P])
        st = sb("st", [P, GT, 6])
        mv = sb("mv", [P, GT, 2])
        ve = sb("ve", [P, GT])
        rstd = sb("rstd", [P, GT])
        xt = sb("xt", [P, GT, F])
        x1n = sb("x1n", [P, GT, F])
        combn = sb("combn", [P, GT, E])
        yacc, ot, num = (stage[:, i * GW:(i + 1) * GW].rearrange("p (b f) -> p b f", f=F) for i in range(3))
        combc = sb("combc", [P, GT, E])
        xnT = sb("xnT", [P, GW])
        x_hi = sb("x_hi", [P, GW], fp16)
        x_lo = sb("x_lo", [P, GW], fp16)
        xn = sb("xn", [P, GT, F])
        den = sb("den", [P, GT])
        emp = sb("emp", [P, GT])
        den1 = sb("den1", [P, GT])
        rden = sb("rden", [P, GT])
        gs = sb("gs", [P, GT, E])
        m8 = sb("m8", [P, GT, 8])
        ix = sb("ix", [P, GT, 8], u32)
        ixf = sb("ixf", [P, GT, 2])
        gd = sb("gd", [P, GT])
        ed = sb("ed", [P, GT])
        eq = sb("eq", [P, GT])
        p1 = sb("p1", [P, GT])
        p2 = sb("p2", [P, GT])
        c1 = sb("c1", [P, GT, E])
        c2 = sb("c2", [P, GT, E])
        combT = sb("combT", [E, GW])
        idle = sb("idle", [1, 4])

        acc = [pb(f"acc{i}") for i in range(2)]
        hps = [pb(f"hps{i}") for i in range(2)]
        yps = [pb(f"yps{i}") for i in range(2)]
        m1 = pb("m1")
        m2 = pb("m2")

        s_wa = sem("s_wa")
        s_we = sem("s_we")
        s_w1 = sem("s_w1")
        s_w2 = sem("s_w2")
        s_xin = [sem(f"s_xin{i}") for i in range(GROUPS)]
        s_adj = [sem(f"s_adj{i}") for i in range(4)]
        s_xt = sem("s_xt")
        s_zero = sem("s_zero")
        s_const = sem("s_const")
        s_pl = sem("s_pl")
        s_ve = sem("s_ve")
        s_rstd = sem("s_rstd")
        s_xh = sem("s_xh")
        s_t0 = sem("s_t0")
        s_hT = sem("s_hT")
        s_WT = sem("s_WT")
        s_WTs = sem("s_WTs")
        s_wam = sem("s_wam")
        s_was = sem("s_was")
        s_wh = sem("s_wh")
        s_whs = sem("s_whs")
        s_ts = sem("s_ts")
        s_tse = sem("s_tse")
        s_sbc = sem("s_sbc")
        s_pre = sem("s_pre")
        s_tm = sem("s_tm")
        s_tmax = sem("s_tmax")
        s_bias0 = sem("s_bias0")
        s_BD = sem("s_BD")
        s_split = sem("s_split")
        s_whi = sem("s_whi")
        s_w2hi = sem("s_w2hi")
        s_wsc = sem("s_wsc")
        s_whm = sem("s_whm")
        s_whx = sem("s_whx")
        s_cexp = sem("s_cexp")
        s_hs = sem("s_hs")
        s_G = sem("s_G")
        s_cg = sem("s_cg")
        s_scaled = sem("s_scaled")
        s_P = sem("s_P")
        s_at = sem("s_at")
        s_fin = sem("s_fin")
        s_num = sem("s_num")
        s_x1 = sem("s_x1")
        s_xn = sem("s_xn")
        s_xtp = sem("s_xtp")
        s_xnt = sem("s_xnt")
        s_xhi = sem("s_xhi")
        s_xlo = sem("s_xlo")
        s_gate = sem("s_gate")
        s_gd = sem("s_gd")
        s_ed = sem("s_ed")
        s_comb = sem("s_comb")
        s_ctp = sem("s_ctp")
        s_cT = sem("s_cT")
        s_bias = sem("s_bias")
        s_res = sem("s_res")
        s_cpc = sem("s_cpc")
        s_h = sem("s_h")
        s_r = sem("s_r")
        s_hi = sem("s_hi")
        s_lo = sem("s_lo")
        s_y = sem("s_y")
        s_cb = sem("s_cb")
        s_out = sem("s_out")
        s_narrow = sem("s_narrow")
        s_pre_adj = [sem(f"s_pre_adj{i}") for i in range(2)]
        s_vl = sem("s_vl")
        s_vmax = sem("s_vmax")
        s_wl = sem("s_wl")
        s_w = sem("s_w")

        def ge(eng, s, value):
            if not (isinstance(value, int) and value <= 0):
                eng.wait_ge(s, value)

        def bodies(eng, steps):
            steps(-1)
            steps(0)
            steps(1)
            with eng.Fori(2, GROUPS - 1) as g:
                steps(g)
            steps(GROUPS - 1)
            steps(GROUPS)
            steps(GROUPS + 1)

        def is_group(g):
            return not isinstance(g, int) or 0 <= g < GROUPS

        def unit(g, rr, c):
            if c >= CH:
                rr, c = rr + c // CH, c % CH
            if rr > GT:
                g, rr = g + 1, rr - GT
            return (g + 1, c) if rr == GT else (g, CH * rr + c)

        block = ctx.enter_context(nc.Block())

        @block.sync
        def _(sp):
            xv = x.rearrange("(c p) f -> p c f", p=P)
            for g in range(GROUPS):
                sp.dma_start(xin[:, GT * g:GT * (g + 1), :], xv[:, GT * g:GT * (g + 1), :]).then_inc(s_xin[g], 16)
                if g == 0:
                    sp.dma_start(W_sb[:, :], W).then_inc(s_wa, 16)
                    sp.dma_start(a_sb[:, 0:1], a[0:F, :]).then_inc(s_wa, 16)
                    sp.dma_start(a_sb[:, 1:2], a[F:2 * F, :]).then_inc(s_wa, 16)
                    sp.dma_start(Wb_row[:, :], Wb[0:1, :].broadcast_to([P, F])).then_inc(s_wa, 16)
                    sp.dma_start(Wb_col[:, :], Wb.rearrange("a f -> f a")).then_inc(s_wa, 16)

            def load_adj(g, n):
                if n >= 4 or not (isinstance(g, int) and g == 0):
                    sp.wait_ge(s_P, 2 * (LOADS * g + n - 3))
                sp.dma_start(adj_sb[n % 4][:, :, :],
                             adjT[bass.ds(P * g, P), ADJ * n:ADJ * (n + 1), :]).then_inc(s_adj[n % 4], 16)

            def load_x(g):
                ge(sp, s_x1, g)
                sp.dma_start(xt[:, :, :], x[bass.ds(g * GW, GW), :].rearrange("(c p) f -> p c f", p=P))\
                    .then_inc(s_xt, 16)

            def store_group(n):
                sp.wait_ge(s_cb, E * (n + 1))
                sp.dma_start(out[bass.ds(n * GW, GW), :].rearrange("(c p) f -> p c f", p=P),
                             ot[:, :, :]).then_inc(s_out, 16)

            for n in range(4):
                load_adj(0, n)
            sp.dma_start(m_bc[:, :], w2.rearrange("p e k f -> p (e k f)")).then_inc(s_w2, 16)
            sp.dma_start(WgT_sb[:, :], WgT).then_inc(s_we, 16)
            sp.dma_start(bg_bc[:, :], bg[0:1, :].broadcast_to([P, E])).then_inc(s_we, 16)
            sp.dma_start(b1_sb[:, :], b1).then_inc(s_we, 16)
            sp.dma_start(b2_sb[:, :], b2).then_inc(s_we, 16)
            load_x(0)
            sp.wait_ge(s_xh, GROUPS)
            sp.dma_start(stage[:, :], w1).then_inc(s_w1, 16)
            sp.wait_ge(s_narrow, 1)
            fast = sp.value_load(narrow[0:1, 0:1])
            with sp.If(fast == 0):
                def load_pre(g):
                    for n in range(LOADS):
                        if n >= 2 or not isinstance(g, int):
                            sp.wait_ge(s_vl, 2 + 2 * ADJ * (LOADS * g + n - 1))
                        sp.dma_start(adj_pre[n % 2][:, :, :],
                                     adjT[bass.ds(P * g, P), ADJ * n:ADJ * (n + 1), :]).then_inc(s_pre_adj[n % 2], 16)

                load_pre(0)
                with sp.Fori(1, GROUPS) as g:
                    load_pre(g)
                sp.wait_ge(s_split, 2)
                sp.dma_start(stage[:, :], w2.rearrange("p e k f -> p (e k f)")).then_inc(s_w2, 16)
            for n in range(4, LOADS):
                load_adj(0, n)
            for g in (1,):
                for n in range(LOADS):
                    load_adj(g, n)
                    if n == 1:
                        load_x(g)
            with sp.Fori(2, GROUPS) as g:
                for n in range(LOADS):
                    load_adj(g, n)
                    if n == 1:
                        load_x(g)
                    if n == 4:
                        store_group(g - 2)
            store_group(GROUPS - 2)
            store_group(GROUPS - 1)
            sp.wait_ge(s_out, 16 * GROUPS)

        @block.gpsimd
        def _(pool):
            nc.gpsimd.memset(ident[:, :], 0.0).then_inc(s_zero, 1)
            nc.gpsimd.memset(mhalf[:, :], -0.5).then_inc(s_zero, 1)
            pool.wait_ge(s_zero, 2)
            nc.gpsimd.affine_select(out=ident[:, :], in_=ident[:, :], compare_op=ALU.not_equal, fill=1.0,
                                    base=0, pattern=[[-1, P]], channel_multiplier=1).then_inc(s_const, 1)
            nc.gpsimd.memset(ones[:, :], 1.0).then_inc(s_const, 1)
            nc.gpsimd.iota(lane[:, :], [[1, E]], base=0, channel_multiplier=0,
                           allow_small_or_imprecise_dtypes=True).then_inc(s_const, 1)
            for g in range(GROUPS):
                pool.wait_ge(s_ve, g + 1)
                nc.gpsimd.tensor_tensor(rs0[:, g * GT:(g + 1) * GT], ve0[:, g * GT:(g + 1) * GT], mhalf[:, :],
                                        ALU.pow).then_inc(s_rstd, 1)
            pool.wait_ge(s_tm, 1)
            nc.gpsimd.partition_all_reduce(tends[:, :], tm_p[:, :], P, bass.bass_isa.ReduceOp.max).then_inc(s_tmax, 1)
            pool.wait_ge(s_wsc, 4)
            nc.gpsimd.tensor_tensor(w2_lo[:, :, :, :].rearrange("p e k f -> p (e k f)"), m_bc[:, :],
                                    w2_hi[:, :, :, :].rearrange("p e k f -> p (e k f)"),
                                    ALU.subtract).then_inc(s_split, 1)
            pool.wait_ge(s_narrow, 1)
            fast = pool.value_load(narrow[0:1, 0:1])
            with pool.If(fast == 0):
                pool.wait_ge(s_split, 1)
                for g in range(GROUPS):
                    pool.wait_ge(s_vl, 2 + 2 * TILES * (g + 1))
                    nc.gpsimd.partition_all_reduce(m_bc[:, g * GW:(g + 1) * GW], vrun[:, :], P,
                                                   bass.bass_isa.ReduceOp.max).then_inc(s_vmax, 1)
            pool.wait_ge(s_wsc, 8)
            nc.gpsimd.tensor_tensor(w1_lo[:, :], stage[:, :], w1_hi[:, :], ALU.subtract).then_inc(s_split, 1)
            with pool.Fori(GROUPS, 2 * GROUPS) as g:
                pool.wait_ge(s_ve, g + 1)
                nc.gpsimd.tensor_tensor(rstd[:, :], ve[:, :], mhalf[:, :], ALU.pow).then_inc(s_rstd, 1)

        @block.vector
        def _(dve):
            links = [0]

            def link(ins):
                links[0] += 1
                ins.then_inc(s_pl, 1)
                dve.wait_ge(s_pl, links[0])

            nc.vector.memset(Wh[:, :, F:FW], 1.0).then_inc(s_pre, 1)
            nc.vector.memset(idle[:, 1:2], 0.0).then_inc(s_pre, 1)

            def mark(ins):
                links[0] += 1
                ins.then_inc(s_pl, 1)
                return links[0]

            def normalise(g):
                dve.wait_ge(s_rstd, g + 1)
                if g >= 2:
                    dve.wait_ge(s_t0, g - 1)
                for u in range(GT * g, GT * (g + 1)):
                    ins = nc.vector.tensor_scalar(xh[g % 2][:, u % GT, :], xin[:, u, :], mv0[:, u, 0:1],
                                                  rs0[:, u:u + 1], ALU.subtract, ALU.mult)
                ins.then_inc(s_xh, 1)

            def keep_Wh(g):
                dve.wait_ge(s_wh, g + 1)
                last = nc.vector.tensor_tensor(Wh[:, GT * g:GT * (g + 1), 0:F],
                                               yps[g % 2][:, :].rearrange("p (b f) -> p b f", f=F),
                                               Wb_row[:, :].unsqueeze(1).broadcast_to([P, GT, F]), ALU.add)
                last.then_inc(s_whs, 1)

            for i in range(GROUPS + 3):
                mine = range(GT * i, GT * (i + 1))
                if i < GROUPS:
                    dve.wait_ge(s_xin[i], 16)
                    for u in mine:
                        last = nc.vector.bn_stats(st0[:, u, :], xin[:, u, :])
                    summed = mark(last)
                if 1 <= i <= GROUPS:
                    normalise(i - 1)
                if i < GROUPS:
                    dve.wait_ge(s_pl, summed)
                    for u in mine:
                        last = nc.vector.bn_aggr(mv0[:, u, :], st0[:, u, :])
                    link(last)
                    nc.vector.tensor_scalar(ve0[:, mine.start:mine.stop], mv0[:, mine.start:mine.stop, 1], EPS, None,
                                            ALU.add).then_inc(s_ve, 1)
                if i == 0:
                    dve.wait_ge(s_const, 3)
                    dve.wait_ge(s_wa, 80)
                    nc.vector.tensor_scalar(a12_bc, ones[:, :], a_sb[:, 0:1], a_sb[:, 1:2], ALU.mult,
                                            ALU.add).then_inc(s_pre, 1)
                if i == 1:
                    dve.wait_ge(s_wam, 1)
                    link(nc.vector.tensor_copy(wa[:, :], m1[:, P:P + 3]))
                    nc.vector.tensor_scalar(wa1_bc[:, :], ones[:, :], wa[:, 0:1], None, ALU.mult).then_inc(s_was, 1)
                if i >= 3:
                    keep_Wh(i - 3)
            dve.wait_ge(s_ts, GROUPS)
            nc.vector.tensor_copy(t_col[:, :], m2[:, 0:TILES])
            nc.vector.tensor_scalar(tneg[:, :], m2[:, 0:TILES], -1.0, None, ALU.mult).then_inc(s_tse, 1)
            dve.wait_ge(s_tse, 1)
            nc.vector.tensor_reduce(tm_p[:, 0:1], t_col[:, :], X, ALU.max)
            nc.vector.tensor_reduce(tm_p[:, 1:2], tneg[:, :], X, ALU.max).then_inc(s_tm, 1)
            dve.wait_ge(s_hT, GROUPS)
            link(nc.vector.tensor_reduce(hsum[:, :], hsum8[:, :], X, ALU.add))
            nc.vector.tensor_scalar(hsum_bc[:, :], ones[:, :], hsum[:, :], None, ALU.mult).then_inc(s_hs, 1)
            dve.wait_ge(s_tmax, 1)
            nc.vector.tensor_scalar(bE[:, :], tmax, -(1.0 - SLOPE), None, ALU.mult)
            nc.vector.tensor_scalar(bD[:, :], tmax, -SLOPE, None, ALU.mult)
            nc.vector.tensor_scalar(bC[:, :], tmax, -(1.0 - SLOPE), None, ALU.mult).then_inc(s_bias0, 1)
            link(nc.vector.tensor_tensor(tmin[:, :], tends[:, 0:1], tends[:, 1:2], ALU.add))
            nc.vector.tensor_scalar(narrow[:, :], tmin[:, :], RANGE, None, ALU.is_le).then_inc(s_narrow, 1)
            dve.wait_ge(s_whx, 1)
            nc.vector.scalar_tensor_tensor(whsum[:, :], Wb_row[:, :], float(N), m1[:, 0:F], op0=ALU.mult,
                                           op1=ALU.add).then_inc(s_whm, 1)

            def group_row(g):
                dve.wait_ge(s_cexp, g + 1)
                ge(dve, s_P, PAIRS * g)
                nc.vector.tensor_scalar(c_g[:, :], cexp[:, :], 1.0, None, ALU.min).then_inc(s_cg, 1)

            def row_maxima():
                dve.wait_ge(s_narrow, 1)
                dve.wait_ge(s_split, 1)
                nc.vector.tensor_scalar(tmin[:, :], tends[:, 1:2], -1.0, None, ALU.mult).then_inc(s_vl, 1)
                dve.wait_ge(s_vl, 1)
                nc.vector.tensor_scalar(v_col[:, :], t_col[:, :], tmin[:, :], None, ALU.subtract).then_inc(s_vl, 1)
                dve.wait_ge(s_vl, 2)
                with dve.Fori(0, GROUPS) as g:
                    for u in range(TILES):
                        n = 2 + 2 * TILES * g + 2 * u
                        if u % ADJ == 0:
                            k = u // ADJ
                            dve.wait_ge(s_pre_adj[k % 2], 16 * (LOADS // 2 * g + k // 2 + 1))
                        dve.wait_ge(s_vl, n)
                        nc.vector.tensor_scalar(vmask[:, :], adj_pre[u // ADJ % 2][:, u % ADJ, :], 0.0,
                                                v_col[:, u:u + 1], ALU.is_gt, ALU.mult).then_inc(s_vl, 1)
                        dve.wait_ge(s_vl, n + 1)
                        if u == 0:
                            nc.vector.tensor_copy(vrun[:, :], vmask[:, :]).then_inc(s_vl, 1)
                        else:
                            nc.vector.tensor_tensor(vrun[:, :], vrun[:, :], vmask[:, :], ALU.max).then_inc(s_vl, 1)
                    dve.wait_ge(s_vmax, g + 1)
                n = 2 + 2 * TILES * GROUPS
                nc.vector.scalar_tensor_tensor(m_bc[:, :], m_bc[:, :], tmin[:, :], s_bc[:, :], op0=ALU.add,
                                               op1=ALU.add).then_inc(s_vl, 1)
                dve.wait_ge(s_vl, n + 1)
                nc.vector.scalar_tensor_tensor(m_bc[:, :], m_bc[:, :], SLOPE, m_bc[:, :], op0=ALU.mult,
                                               op1=ALU.max).then_inc(s_vl, 1)
                dve.wait_ge(s_vl, n + 2)

            def make_logits(g, rr, c):
                g, u = unit(g, rr, c)
                if not is_group(g):
                    return
                n = PAIRS * g + u // 2
                Gp = G[u // 2 % 4]
                ge(dve, s_P, n - 3)
                for k in range(2):
                    last = nc.vector.tensor_scalar(Gp[:, k, :], s_bc[:, bass.ds(g * GW, GW)], t_col[:, u + k:u + k + 1],
                                                   None, ALU.add)
                last.then_inc(s_wl, 1)
                dve.wait_ge(s_wl, 3 * n + 1)
                nc.vector.scalar_tensor_tensor(Gp[:, :, :], Gp[:, :, :], SLOPE, Gp[:, :, :], op0=ALU.mult,
                                               op1=ALU.max).then_inc(s_wl, 1)
                dve.wait_ge(s_wl, 3 * n + 2)
                for k in range(2):
                    last = nc.vector.tensor_tensor(Gp[:, k, :], Gp[:, k, :], m_bc[:, bass.ds(g * GW, GW)], ALU.subtract)
                last.then_inc(s_wl, 1)
                dve.wait_ge(s_wl, 3 * n + 3)
                nc.vector.tensor_scalar(Gp[:, :, :], Gp[:, :, :], TOP, None, ALU.min).then_inc(s_w, 1)

            def scale_Wh(q):
                tiles = slice(CH * q, CH * (q + 1))
                nc.vector.tensor_tensor(Wh[:, tiles, :], Wh[:, tiles, :],
                                        D_col[:, tiles].unsqueeze(2).broadcast_to([P, CH, FW]),
                                        ALU.mult).then_inc(s_scaled, 1)

            def weigh(g, rr, c):
                g, u = unit(g, rr, c)
                if not is_group(g):
                    return
                n = PAIRS * g + u // 2
                if u == 0:
                    group_row(g)
                    dve.wait_ge(s_cg, g + 1)
                if isinstance(g, int) and g == 0 and u % CH == 0:
                    scale_Wh(u // CH)
                dve.wait_ge(s_G, n + 1)
                ge(dve, s_at, 2 * (n - 3))
                for k in range(2):
                    last = nc.vector.scalar_tensor_tensor(prob[u // 2 % 4][:, k, :], c_g[:, :], E_col[:, u + k:u + k + 1],
                                                          G[u // 2 % 4][:, k, :], op0=ALU.max, op1=ALU.min)
                last.then_inc(s_P, 1)

            def make_P(g, rr, c):
                g, u = unit(g, rr, c)
                if not is_group(g):
                    return
                n = PAIRS * g + u // 2
                k = u // ADJ
                if u % ADJ == 0:
                    dve.wait_ge(s_adj[k % 4], 16 * (LOADS // 4 * g + k // 4 + 1))
                dve.wait_ge(s_G, n + 1)
                ge(dve, s_at, 2 * (n - 3))
                nc.vector.scalar_tensor_tensor(prob[u // 2 % 4][:, :, :], adj_sb[k % 4][:, u % ADJ:u % ADJ + 2, :],
                                               0.0, G[u // 2 % 4][:, :, :], op0=ALU.is_gt,
                                               op1=ALU.mult).then_inc(s_P, 1)

            def low_part(g, e, k):
                n = KH * (E * (g - 1) + e) + k
                dve.wait_ge(s_hi, n + 1)
                ge(dve, s_y, n - 2 * KH + 1)
                nc.vector.tensor_tensor(h_lo[e % 2][:, k, :], r[k][:, :], h_hi[e % 2][:, k, :],
                                        ALU.subtract).then_inc(s_lo, 1)

            def combine(g, e):
                n = E * (g - 1) + e
                dve.wait_ge(s_y, KH * (n + 1))
                ge(dve, s_cb, n)
                if e == 0:
                    dve.wait_ge(s_cpc, g)
                if e == E - 1:
                    ge(dve, s_out, 16 * (g - 1))
                dst = ot if e == E - 1 else yacc
                for b in range(GT):
                    last = nc.vector.scalar_tensor_tensor(
                        dst[:, b, :], yps[e % 2][:, b * P:(b + 1) * P], combc[:, b, e:e + 1],
                        yacc[:, b, :], op0=ALU.mult, op1=ALU.add)
                last.then_inc(s_cb, 1)

            def hand_over(g):
                dve.wait_ge(s_res, g + 1)
                dve.wait_ge(s_comb, g + 1)
                dve.wait_ge(s_split, 2)
                ge(dve, s_cb, E * g)
                nc.vector.tensor_copy(yacc[:, :, :], x1n[:, :, :])
                nc.vector.tensor_scalar(combc[:, :, :], combn[:, :, :], 1.0 / WS, None, ALU.mult).then_inc(s_cpc, 1)

            def bc(ap, n):
                return ap.unsqueeze(2).broadcast_to([P, GT, n])

            def finish(g, part):
                def after(k):
                    dve.wait_ge(s_fin, NFIN * g + k)

                if part == 1:
                    dve.wait_ge(s_split, 2)
                    dve.wait_ge(s_at, TILES * (g + 1))
                    for i in range(2):
                        ins = nc.vector.tensor_copy(den[:, 2 * i:2 * i + 2], acc[i][:, F:F + FW + 1:FW])
                    ins.then_inc(s_fin, 1)
                    after(1)
                    nc.vector.tensor_scalar(emp[:, :], den[:, :], 0.0, None, ALU.is_equal).then_inc(s_fin, 1)
                    after(2)
                    nc.vector.scalar_tensor_tensor(den1[:, :], emp[:, :], float(N), den[:, :], op0=ALU.mult,
                                                   op1=ALU.add).then_inc(s_fin, 1)
                    for b in range(GT):
                        ins = nc.vector.scalar_tensor_tensor(
                            num[:, b, :], whsum[:, :], emp[:, b:b + 1], acc[b // 2][:, b % 2 * FW:b % 2 * FW + F],
                            op0=ALU.mult, op1=ALU.add)
                    ins.then_inc(s_num, 1)
                    after(3)
                    nc.vector.reciprocal(rden[:, :], den1[:, :]).then_inc(s_fin, 1)
                    after(4)
                    dve.wait_ge(s_num, g + 1)
                    dve.wait_ge(s_xt, 16 * (g + 1))
                    for b in range(GT):
                        ins = nc.vector.scalar_tensor_tensor(x1n[:, b, :], num[:, b, :], rden[:, b:b + 1],
                                                             xt[:, b, :], op0=ALU.mult, op1=ALU.add)
                    ins.then_inc(s_x1, 1)
                if part == 2:
                    dve.wait_ge(s_x1, g + 1)
                    for b in range(GT):
                        ins = nc.vector.bn_stats(st[:, b, :], x1n[:, b, :])
                    ins.then_inc(s_fin, 1)
                    after(5)
                    nc.vector.memset(idle[:, 3:4], 0.0)
                    for b in range(GT):
                        ins = nc.vector.bn_aggr(mv[:, b, :], st[:, b, :])
                    ins.then_inc(s_fin, 1)
                    after(6)
                    nc.vector.tensor_scalar(ve[:, :], mv[:, :, 1], EPS, None, ALU.add).then_inc(s_ve, 1)
                if part == 3:
                    dve.wait_ge(s_rstd, GROUPS + g + 1)
                    ge(dve, s_xtp, g)
                    for b in range(GT):
                        ins = nc.vector.tensor_scalar(xn[:, b, :], x1n[:, b, :], mv[:, b, 0:1], rstd[:, b:b + 1],
                                                      ALU.subtract, ALU.mult)
                    ins.then_inc(s_xn, 1)
                if part == 6:
                    dve.wait_ge(s_gate, g + 1)
                    nc.vector.tensor_tensor(gs[:, :, :], m2[:, 0:GT * E].rearrange("p (b e) -> p b e", e=E),
                                            bg_bc[:, :].unsqueeze(1).broadcast_to([P, GT, E]),
                                            ALU.add).then_inc(s_fin, 1)
                    after(7)
                    nc.vector.memset(idle[:, 3:4], 0.0)
                    for b in range(GT):
                        ins = nc.vector.max(m8[:, b, :], gs[:, b, :])
                    ins.then_inc(s_fin, 1)
                    after(8)
                    nc.vector.tensor_tensor(gd[:, :], m8[:, :, 1], m8[:, :, 0], ALU.subtract).then_inc(s_gd, 1)
                    for b in range(GT):
                        ins = nc.vector.max_index(ix[:, b, :], m8[:, b, :], gs[:, b, :])
                    ins.then_inc(s_fin, 1)
                    after(9)
                    nc.vector.tensor_copy(ixf[:, :, :], ix[:, :, 0:2]).then_inc(s_fin, 1)
                if part == 7:
                    dve.wait_ge(s_ed, g + 1)
                    nc.vector.tensor_scalar(eq[:, :], ed[:, :], 1.0, None, ALU.add).then_inc(s_fin, 1)
                    after(11)
                    nc.vector.reciprocal(p1[:, :], eq[:, :]).then_inc(s_fin, 1)
                    after(12)
                    nc.vector.tensor_tensor(p2[:, :], ed[:, :], p1[:, :], ALU.mult).then_inc(s_fin, 1)
                    after(13)
                    for b in range(GT):
                        nc.vector.tensor_scalar(c1[:, b, :], lane[:, :], ixf[:, b, 0:1], p1[:, b:b + 1],
                                                ALU.is_equal, ALU.mult)
                    for b in range(GT):
                        ins = nc.vector.tensor_scalar(c2[:, b, :], lane[:, :], ixf[:, b, 1:2], p2[:, b:b + 1],
                                                      ALU.is_equal, ALU.mult)
                    ins.then_inc(s_fin, 1)
                    after(14)
                    nc.vector.tensor_tensor(combn[:, :, :], c1[:, :, :], c2[:, :, :], ALU.add).then_inc(s_comb, 1)

            def residual(g):
                dve.wait_ge(s_bias, g + 1)
                nc.vector.tensor_tensor(x1n[:, :, :], x1n[:, :, :],
                                        m1[:, :].rearrange("p (b f) -> p b f", f=F), ALU.add).then_inc(s_res, 1)

            def steps(g, ahead, weigh):
                ffn = not isinstance(g, int) or 1 <= g <= GROUPS
                for rr in range(1, GT + 1):
                    e0 = 2 * (rr - 1)
                    for c in range(CH):
                        if c % 2 == 0:
                            if ahead:
                                ahead(g, rr, c + 4)
                            weigh(g, rr, c + 2)
                        if ffn and (c >= LAG or rr > 1):
                            e, k = divmod(KH * e0 + c - LAG, KH)
                            low_part(g, e, k)
                        if rr == 1:
                            if is_group(g - 1) and c == 3:
                                residual(g - 1)
                            if is_group(g - 2) and c in (1, 3):
                                combine(g - 1, E - 2 + c // 2)
                            if is_group(g - 1) and c == 5:
                                hand_over(g - 1)
                        if is_group(g) and rr == GT:
                            finish(g, c)
                        if ffn and rr > 1 and c in (1, 5):
                            combine(g, e0 - 2 + c // 4)
                if ffn:
                    for k in range(KH - LAG, KH):
                        low_part(g, E - 1, k)
                if is_group(g):
                    dve.wait_ge(s_xhi, g + 1)
                    nc.vector.tensor_tensor(x_lo[:, :], xnT[:, :], x_hi[:, :], ALU.subtract).then_inc(s_xlo, 1)

            def program(ahead, weigh):
                if ahead:
                    ahead(-1, GT, 0)
                    dve.wait_ge(s_w2hi, 1)
                    ahead(-1, GT, 2)
                weigh(-1, GT, 0)

                def schedule(g):
                    if isinstance(g, int) and g == -1:
                        for c in range(0, CH, 2):
                            if ahead:
                                ahead(g, GT, c + 4)
                            weigh(g, GT, c + 2)
                    else:
                        steps(g, ahead, weigh)

                bodies(dve, schedule)

            dve.wait_ge(s_narrow, 1)
            fast = dve.value_load(narrow[0:1, 0:1])
            dve.wait_ge(s_BD, 2)
            before = links[0]
            with dve.If(fast != 0):
                program(None, weigh)
            with dve.Else():
                links[0] = before
                row_maxima()
                nc.vector.memset(idle[:, 2:3], 0.0).then_inc(s_scaled, STEPS)
                program(make_logits, make_P)

        @block.scalar
        def _(act):
            def split(n, q):
                if q == 0:
                    act.wait_ge((s_w2, s_w1)[n], 16)
                hi = (w2_hi[:, :, :, :].rearrange("p e k f -> p (e k f)"), w1_hi[:, :])[n]
                src = (m_bc, stage)[n]
                cols = slice(q * E * HID // 4, (q + 1) * E * HID // 4)
                nc.scalar.activation(hi[:, cols], src[:, cols], ACT.Copy, scale=WS).then_inc(s_whi, 1)
                act.wait_ge(s_whi, 4 * n + q + 1)
                nc.scalar.activation(src[:, cols], src[:, cols], ACT.Copy, scale=WS).then_inc(s_wsc, 1)

            act.wait_ge(s_WT, 1)
            nc.scalar.activation(WT, m1[:, 0:P], ACT.Copy).then_inc(s_WTs, 1)
            for i in range(GROUPS + 2):
                if i < GROUPS:
                    act.wait_ge(s_t0, i + 1)
                    if i >= 2:
                        act.wait_ge(s_ts, i - 1)
                    nc.scalar.activation(hT[i % 2], hps[i % 2][:, :], ACT.Copy,
                                         accum_out=hsum8[:, i:i + 1]).then_inc(s_hT, 1)
                if i >= 2:
                    g = i - 2
                    act.wait_ge(s_ts, g + 1)
                    nc.scalar.activation(s_bc[:, g * GW:(g + 1) * GW], acc[g % 2][:, :], ACT.Identity,
                                         bias=wa[:, 2:3]).then_inc(s_sbc, 1)
                if 4 <= i < 8:
                    split(0, i - 4)
            act.wait_ge(s_bias0, 1)
            nc.scalar.activation(D_col[:, :], t_col[:, :], ACT.Exp, bias=bD[:, :], scale=SLOPE).then_inc(s_BD, 1)
            nc.scalar.activation(E_col[:, :], t_col[:, :], ACT.Exp, bias=bE[:, :],
                                 scale=1.0 - SLOPE).then_inc(s_BD, 1)
            act.wait_ge(s_sbc, GROUPS)

            def group_row(g):
                ge(act, s_cg, g)
                nc.scalar.activation(idle[:, 0:1], idle[:, 1:2], ACT.Copy)
                nc.scalar.activation(cexp[:, :], s_bc[:, bass.ds(g * GW, GW)], ACT.Exp, bias=bC[:, :],
                                     scale=-(1.0 - SLOPE)).then_inc(s_cexp, 1)

            def edges(g, rr, c):
                g, u = unit(g, rr, c)
                if not is_group(g):
                    return
                n, k = PAIRS * g + u // 2, u // ADJ
                if u % ADJ == 0:
                    act.wait_ge(s_adj[k % 4], 16 * (LOADS // 4 * g + k // 4 + 1))
                ge(act, s_P, n - 3)
                nc.scalar.activation(G[u // 2 % 4][:, :, :], adj_sb[k % 4][:, u % ADJ:u % ADJ + 2, :],
                                     ACT.Relu).then_inc(s_G, 1)

            def raise_pair(g, rr, c):
                g, u = unit(g, rr, c)
                if not is_group(g):
                    return
                act.wait_ge(s_w, PAIRS * g + u // 2 + 1)
                nc.scalar.activation(G[u // 2 % 4][:, :, :], G[u // 2 % 4][:, :, :], ACT.Exp).then_inc(s_G, 1)

            def relu(g, e, k):
                n = KH * (E * (g - 1) + e) + k
                act.wait_ge(s_h, n + 1)
                ge(act, s_lo, n - KH + 1)
                nc.scalar.activation(r[k][:, :], hps[k % 2][:, :], ACT.Relu, scale=1.0 / WS,
                                     bias=b1_sb[:, KH * e + k:KH * e + k + 1]).then_inc(s_r, 1)

            def high_part(g, e, k):
                n = KH * (E * (g - 1) + e) + k
                act.wait_ge(s_r, n + 1)
                ge(act, s_y, n - 2 * KH + 1)
                nc.scalar.activation(h_hi[e % 2][:, k, :], r[k][:, :], ACT.Copy).then_inc(s_hi, 1)

            def finish(g, part):
                if part == 4:
                    act.wait_ge(s_xtp, g + 1)
                    ge(act, s_xlo, g)
                    nc.scalar.activation(xnT[:, :], m1[:, :], ACT.Copy).then_inc(s_xnt, 1)
                if part == 6:
                    act.wait_ge(s_gd, g + 1)
                    nc.scalar.activation(ed[:, :], gd[:, :], ACT.Exp).then_inc(s_ed, 1)
                if part == CH:
                    act.wait_ge(s_ctp, g + 1)
                    nc.scalar.activation(combT[:, :], m2[0:E, :], ACT.Copy).then_inc(s_cT, 1)

            def steps(g, general):
                ffn = not isinstance(g, int) or 1 <= g <= GROUPS
                for rr in range(1, GT + 1):
                    e0 = 2 * (rr - 1)
                    for c in range(CH):
                        if c % 2 == 0 and (rr == GT or not isinstance(g, int) or g >= 0):
                            (raise_pair if general else edges)(g, rr, c + 4)
                        if not general and isinstance(g, int) and g == 0 and rr <= 2 and c % 4 == 1:
                            split(1, 2 * (rr - 1) + c // 4)
                        if ffn:
                            relu(g, e0 + c // KH, c % KH)
                        if ffn:
                            high_part(g, e0 + c // KH, c % KH)
                        if is_group(g) and rr == GT:
                            finish(g, c)
                        if is_group(g - 1) and rr == 1 and c == 1:
                            finish(g - 1, CH)
                    if not general and rr == 2 and is_group(g + 1) and (not isinstance(g, int) or g >= 0):
                        group_row(g + 1)
                if is_group(g):
                    act.wait_ge(s_xnt, g + 1)
                    ge(act, s_h, KH * E * g)
                    nc.scalar.activation(x_hi[:, :], xnT[:, :], ACT.Copy).then_inc(s_xhi, 1)

            act.wait_ge(s_narrow, 1)
            fast = act.value_load(narrow[0:1, 0:1])
            with act.If(fast != 0):
                group_row(0)
                edges(-1, GT, 0)
                edges(-1, GT, 2)
                bodies(act, lambda g: steps(g, False))
            with act.Else():
                raise_pair(-1, GT, 0)
                for q in range(4):
                    split(1, q)
                act.wait_ge(s_w2, 32)
                nc.scalar.activation(w2_hi[:, :, :, :].rearrange("p e k f -> p (e k f)"), stage[:, :], ACT.Copy,
                                     scale=WS).then_inc(s_w2hi, 1)
                raise_pair(-1, GT, 2)
                bodies(act, lambda g: steps(g, True))


        @block.tensor
        def _(pe):
            pe.wait_ge(s_const, 1)
            pe.wait_ge(s_wa, 80)
            nc.tensor.transpose(m1[:, 0:P], W_sb[:, :], ident[:, :]).then_inc(s_WT, 1)
            pe.wait_ge(s_WTs, 1)
            pe.wait_ge(s_pre, 3)
            nc.tensor.matmul(m1[:, P:P + 2], WT, a_sb[:, :], start=True, stop=True)
            nc.tensor.matmul(m1[:, P + 2:P + 3], a12_bc, Wb_col[:, :], start=True, stop=True).then_inc(s_wam, 1)
            for i in range(GROUPS + 1):
                if i < GROUPS:
                    pe.wait_ge(s_xh, i + 1)
                    if i >= 2:
                        pe.wait_ge(s_hT, i - 1)
                    for b in range(GT):
                        last = nc.tensor.transpose(hps[i % 2][:, b * P:(b + 1) * P], xh[i % 2][:, b, :], ident[:, :])
                    last.then_inc(s_t0, 1)
                if i >= 1:
                    g = i - 1
                    pe.wait_ge(s_hT, g + 1)
                    if g >= 2:
                        pe.wait_ge(s_whs, g - 1)
                    for b in range(GT):
                        last = nc.tensor.matmul(yps[g % 2][:, b * P:(b + 1) * P], hT[g % 2][:, b * P:(b + 1) * P],
                                                W_sb[:, :], start=True, stop=True)
                    last.then_inc(s_wh, 1)
                    if g == 0:
                        pe.wait_ge(s_was, 1)
                    if g >= 2:
                        pe.wait_ge(s_sbc, g - 1)
                    nc.tensor.matmul(acc[g % 2][:, :], wa1_bc[:, :], hT[g % 2], start=True, stop=True)
                    for b in range(GT):
                        last = nc.tensor.matmul(m2[:, GT * g + b:GT * g + b + 1], hT[g % 2][:, b * P:(b + 1) * P],
                                                wa[:, 1:2], start=True, stop=True)
                    last.then_inc(s_ts, 1)
            pe.wait_ge(s_hs, 1)
            nc.tensor.matmul(m1[:, 0:F], hsum_bc[:, :], W_sb[:, :], start=True, stop=True).then_inc(s_whx, 1)
            pe.wait_ge(s_sbc, GROUPS)
            pe.wait_ge(s_whs, GROUPS)
            pe.wait_ge(s_we, 64)
            pe.wait_ge(s_tse, 1)

            def attend(g, rr, c):
                g, u = unit(g, rr, c)
                if not is_group(g):
                    return
                n = PAIRS * g + u // 2
                if u == 0:
                    ge(pe, s_num, g)
                if u % 2 == 0:
                    pe.wait_ge(s_P, n + 1)
                if isinstance(g, int) and g == 0 and u % CH == 0:
                    pe.wait_ge(s_scaled, u // CH + 1)
                for b in range(GT):
                    last = nc.tensor.matmul(acc[b // 2][:, b % 2 * FW:b % 2 * FW + FW],
                                            prob[u // 2 % 4][:, u % 2, b * P:(b + 1) * P], Wh[:, u, :],
                                            start=(u == 0 and b % 2 == 0), stop=(u == TILES - 1),
                                            skip_group_check=True)
                last.then_inc(s_at, 1)

            def up(g, e, k):
                n = KH * (E * (g - 1) + e) + k
                if e == 0 and k == 0:
                    pe.wait_ge(s_xlo, g)
                ge(pe, s_r, n - 1)
                j = e * HID + k * P
                nc.tensor.matmul(hps[k % 2][:, :], w1_hi[:, j:j + P], x_hi[:, :], start=True, stop=False)
                nc.tensor.matmul(hps[k % 2][:, :], w1_hi[:, j:j + P], x_lo[:, :], start=False, stop=False)
                nc.tensor.matmul(hps[k % 2][:, :], w1_lo[:, j:j + P], x_hi[:, :], start=False,
                                 stop=True).then_inc(s_h, 1)

            def down(g, e, k):
                n = E * (g - 1) + e
                pe.wait_ge(s_lo, KH * n + k + 1)
                if k == 0:
                    ge(pe, s_cb, n - 1)
                for b in range(GT):
                    dst = yps[e % 2][:, b * P:(b + 1) * P]
                    hi, lo = (v[e % 2][:, k, b * P:(b + 1) * P] for v in (h_hi, h_lo))
                    nc.tensor.matmul(dst, hi, w2_hi[:, e, k, :], start=(k == 0 and b == 0), stop=False,
                                     skip_group_check=True)
                    nc.tensor.matmul(dst, hi, w2_lo[:, e, k, :], start=False, stop=False, skip_group_check=True)
                    last = nc.tensor.matmul(dst, lo, w2_hi[:, e, k, :], start=False, stop=(k == KH - 1),
                                            skip_group_check=True)
                last.then_inc(s_y, 1)

            def finish(g, part):
                if part == 4:
                    pe.wait_ge(s_xn, g + 1)
                    if isinstance(g, int) and g == 0:
                        pe.wait_ge(s_whm, 1)
                    ge(pe, s_res, g)
                    for b in range(GT):
                        last = nc.tensor.transpose(m1[:, b * P:(b + 1) * P], xn[:, b, :], ident[:, :])
                    last.then_inc(s_xtp, 1)
                if part == 5:
                    pe.wait_ge(s_xnt, g + 1)
                    ge(pe, s_cT, g)
                    for b in range(GT):
                        last = nc.tensor.matmul(m2[:, b * E:(b + 1) * E], xnT[:, b * P:(b + 1) * P], WgT_sb[:, :],
                                                start=True, stop=True)
                    last.then_inc(s_gate, 1)
                if part == CH:
                    pe.wait_ge(s_comb, g + 1)
                    for b in range(GT):
                        last = nc.tensor.transpose(m2[0:E, b * P:(b + 1) * P], combn[:, b, :], ident[:, :])
                    last.then_inc(s_ctp, 1)
                if part == CH + 1:
                    pe.wait_ge(s_cT, g + 1)
                    for b in range(GT):
                        last = nc.tensor.matmul(m1[:, b * P:(b + 1) * P], combT[:, b * P:(b + 1) * P], b2_sb[:, :],
                                                start=True, stop=True)
                    last.then_inc(s_bias, 1)

            def steps(g):
                ffn = not isinstance(g, int) or 1 <= g <= GROUPS
                for rr in range(1, GT + 1):
                    e0 = 2 * (rr - 1)
                    for c in range(CH):
                        if ffn:
                            up(g, e0 + c // KH, c % KH)
                        if rr < GT and not (isinstance(g, int) and g < 0):
                            attend(g, rr, c)
                        if rr == GT:
                            for cc in {0: (), 1: (), 2: (0, 1), 3: (2, 3)}.get(c, (c,)):
                                attend(g, rr, cc)
                        if ffn and e0 + c // KH >= 1:
                            down(g, e0 + c // KH - 1, c % KH)
                        if is_group(g) and rr == GT:
                            finish(g, c)
                        if is_group(g - 1) and rr == 1 and c in (0, 2):
                            finish(g - 1, CH + c // 2)
                if ffn:
                    for k in range(KH):
                        down(g, E - 1, k)

            bodies(pe, steps)


_OUT = ((4096, 128), "float32")


def kernel(x, adj, L0_gnn_W_w, L0_gnn_W_b, L0_gnn_a, L0_ffn_Wg, L0_ffn_bg, L0_ffn_W1, L0_ffn_b1,
           L0_ffn_W2, L0_ffn_b2):
    import numpy as np
    import concourse.bacc as bacc
    from concourse import mybir as mb
    from concourse.bass_utils import run_bass_kernel_spmd

    def flat(v):
        return np.ascontiguousarray(v)

    W1, b1, W2 = np.asarray(L0_ffn_W1), np.asarray(L0_ffn_b1), np.asarray(L0_ffn_W2)
    E, HID, F = W1.shape
    N = np.asarray(x).shape[0]
    arrays = {
        "x": flat(x),
        "adjT": flat(np.asarray(adj).reshape(N // 512, 512, N // 128, 128).transpose(0, 3, 2, 1)
                     .reshape(N // 4, N // 128, 512)),
        "W": flat(L0_gnn_W_w),
        "Wb": flat(np.asarray(L0_gnn_W_b).reshape(1, F)),
        "a": flat(L0_gnn_a),
        "WgT": flat(np.asarray(L0_ffn_Wg).T),
        "bg": flat(np.asarray(L0_ffn_bg).reshape(1, E)),
        "w1": flat(W1.transpose(2, 0, 1).reshape(F, E * HID)),
        "b1": flat(b1.reshape(E, HID // 128, 128).transpose(2, 0, 1).reshape(128, -1)),
        "w2": flat(W2.reshape(E, F, HID // 128, 128).transpose(3, 0, 2, 1)),
        "b2": flat(L0_ffn_b2),
    }
    nc = bacc.Bacc("TRN2", target_bir_lowering=False, num_devices=1)
    args = [nc.dram_tensor(k, v.shape, mb.dt.from_np(v.dtype), kind="ExternalInput").ap() for k, v in arrays.items()]
    args.append(nc.dram_tensor("out", _OUT[0], mb.dt.from_np(np.dtype(_OUT[1])), kind="ExternalOutput").ap())
    build(nc, *args)
    r = run_bass_kernel_spmd(nc, [arrays], core_ids=[0])
    return r.results[0]["out"]
```
